# Optimizing a Trainium2 kernel written in Bass

```python
import numpy as np
import jax
import jax.numpy as jnp

def _softmax(x, axis=-1):
    return jax.nn.softmax(x, axis=axis)

def _gelu(x):
    return jax.nn.gelu(x, approximate=True)

def _silu(x):
    return jax.nn.silu(x)

def _sigmoid(x):
    return jax.nn.sigmoid(x)

def _layernorm(x, axis=-1, eps=1e-05):
    m = jnp.mean(x, axis=axis, keepdims=True)
    v = jnp.var(x, axis=axis, keepdims=True)
    return (x - m) / jnp.sqrt(v + eps)

def _scatter_add(tgt, idx, src, axis=0):
    return tgt.at[idx].add(src)

def _segment_sum(src, seg, n):
    return jax.ops.segment_sum(src, seg, n)
kernel_name = 'mk_xattn_seq_d2_seqx_r4_294ca2'

def setup_inputs(seed: int=0):
    np.random.seed(seed)
    _w = jnp.asarray

    def _rec_inputs():
        import jax
        import jax.numpy as jnp
        _rk = jax.random.key(seed)
        x = -0.0001548 + 1 * jax.random.normal(jax.random.fold_in(_rk, 1), (16, 112, 320), jnp.float32)
        _lenS = 112 - jax.random.randint(jax.random.fold_in(_rk, 7), (16,), 0, max(1, 112 // 4) + 1, jnp.int32)
        _lenS2 = 375 - jax.random.randint(jax.random.fold_in(_rk, 8), (16,), 0, max(1, 375 // 4) + 1, jnp.int32)
        _ctx_768P = jax.random.normal(jax.random.fold_in(_rk, 11), (16, 16, 192), jnp.float32)
        _ctx_768c = jax.random.dirichlet(jax.random.fold_in(_rk, 511), 0.3 * jnp.ones((16,), jnp.float32), (16, 375))
        _ctx_768t = jnp.einsum('bsk,bkd->bsd', _ctx_768c, _ctx_768P)
        _ctx_768t = _ctx_768t * jax.lax.rsqrt(jnp.mean(jnp.square(_ctx_768t)) + 1e-12) * 0.953939
        ctx_768 = 0.00141353 + 0.998943 * (_ctx_768t + 0.3 * jax.random.normal(jax.random.fold_in(_rk, 611), (16, 375, 192), jnp.float32))
        return (x, ctx_768)
    x, ctx_768 = _rec_inputs()

    def _L0_xattn_setup():
        import jax, jax.numpy as jnp
        import numpy as np
        HEADS = 8
        NUM_TOKENS = 4
        CROSS_ATTENTION_DIM = 192

        def _mha(q, k, v, heads=HEADS):
            B, Sq, H = q.shape
            Sk = k.shape[1]
            d = H // heads
            qh = q.reshape(B, Sq, heads, d).transpose(0, 2, 1, 3)
            kh = k.reshape(B, Sk, heads, d).transpose(0, 2, 1, 3)
            vh = v.reshape(B, Sk, heads, d).transpose(0, 2, 1, 3)
            scores = jnp.einsum('bhqd,bhkd->bhqk', qh, kh) * jnp.asarray(d, q.dtype) ** (-0.5)
            probs = jax.nn.softmax(scores, axis=-1)
            out = jnp.einsum('bhqk,bhkd->bhqd', probs, vh)
            return out.transpose(0, 2, 1, 3).reshape(B, Sq, H)
        key = jax.random.key(seed)
        ks = jax.random.split(key, 10)
        B, S, H, CAD, T = (4, 256, 320, CROSS_ATTENTION_DIM, NUM_TOKENS)
        sc = 0.02
        return {'hidden_states': jax.random.normal(ks[0], (B, S, H), jnp.float32), 'encoder_hidden_states': jax.random.normal(ks[1], (B, 77 + T, CAD), jnp.float32), 'Wq': jax.random.normal(ks[2], (H, H), jnp.float32) * sc, 'Wk': jax.random.normal(ks[3], (CAD, H), jnp.float32) * sc, 'Wv': jax.random.normal(ks[4], (CAD, H), jnp.float32) * sc, 'Wq_ca': jax.random.normal(ks[5], (T, H), jnp.float32) * sc, 'Wk_ca': jax.random.normal(ks[6], (CAD, H), jnp.float32) * sc, 'Wv_ca': jax.random.normal(ks[7], (CAD, H), jnp.float32) * sc, 'Wout': jax.random.normal(ks[8], (H, H), jnp.float32) * sc, 'b_out': jnp.zeros((H,), jnp.float32)}
    _L0_xattn_all = _L0_xattn_setup()
    _L0_xattn_in = {k: v for k, v in _L0_xattn_all.items() if k in ('Wq', 'Wk', 'Wv', 'Wq_ca', 'Wk_ca', 'Wv_ca', 'Wout', 'b_out')}
    del _L0_xattn_all

    def _L1_xattn_setup():
        import jax, jax.numpy as jnp
        import numpy as np
        HEADS = 20
        NUM_AOE = 16
        NUM_IP = 16
        key = jax.random.key(seed)
        ks = jax.random.split(key, 7)
        B, Sq, H = (8, 1024, 320)
        Skv, C = (109, 192)
        scale = 0.02
        return {'hidden_states': jax.random.normal(ks[0], (B, Sq, H), jnp.float32), 'encoder_hidden_states': jax.random.normal(ks[1], (B, Skv, C), jnp.float32), 'Wq': jax.random.normal(ks[2], (H, H), jnp.float32) * scale, 'Wk': jax.random.normal(ks[3], (C, H), jnp.float32) * scale, 'Wv': jax.random.normal(ks[4], (C, H), jnp.float32) * scale, 'Wo': jax.random.normal(ks[5], (H, H), jnp.float32) * scale, 'bo': jnp.zeros((H,), jnp.float32)}
    _L1_xattn_all = _L1_xattn_setup()
    _L1_xattn_in = {k: v for k, v in _L1_xattn_all.items() if k in ('Wq', 'Wk', 'Wv', 'Wo', 'bo')}
    del _L1_xattn_all
    return {'x': x, 'ctx_768': ctx_768, 'L0_xattn_Wq': _L0_xattn_in['Wq'], 'L0_xattn_Wk': _L0_xattn_in['Wk'], 'L0_xattn_Wv': _L0_xattn_in['Wv'], 'L0_xattn_Wq_ca': _L0_xattn_in['Wq_ca'], 'L0_xattn_Wk_ca': _L0_xattn_in['Wk_ca'], 'L0_xattn_Wv_ca': _L0_xattn_in['Wv_ca'], 'L0_xattn_Wout': _L0_xattn_in['Wout'], 'L0_xattn_b_out': _L0_xattn_in['b_out'], 'L1_xattn_Wq': _L1_xattn_in['Wq'], 'L1_xattn_Wk': _L1_xattn_in['Wk'], 'L1_xattn_Wv': _L1_xattn_in['Wv'], 'L1_xattn_Wo': _L1_xattn_in['Wo'], 'L1_xattn_bo': _L1_xattn_in['bo']}

def reference(x, ctx_768, L0_xattn_Wq, L0_xattn_Wk, L0_xattn_Wv, L0_xattn_Wq_ca, L0_xattn_Wk_ca, L0_xattn_Wv_ca, L0_xattn_Wout, L0_xattn_b_out, L1_xattn_Wq, L1_xattn_Wk, L1_xattn_Wv, L1_xattn_Wo, L1_xattn_bo):
    import jax
    import jax.numpy as jnp

    def _L0_xattn_ref(hidden_states, encoder_hidden_states, Wq, Wk, Wv, Wq_ca, Wk_ca, Wv_ca, Wout, b_out):
        import jax, jax.numpy as jnp
        import numpy as np
        HEADS = 8
        NUM_TOKENS = 4
        CROSS_ATTENTION_DIM = 192

        def _mha(q, k, v, heads=HEADS):
            B, Sq, H = q.shape
            Sk = k.shape[1]
            d = H // heads
            qh = q.reshape(B, Sq, heads, d).transpose(0, 2, 1, 3)
            kh = k.reshape(B, Sk, heads, d).transpose(0, 2, 1, 3)
            vh = v.reshape(B, Sk, heads, d).transpose(0, 2, 1, 3)
            scores = jnp.einsum('bhqd,bhkd->bhqk', qh, kh) * jnp.asarray(d, q.dtype) ** (-0.5)
            probs = jax.nn.softmax(scores, axis=-1)
            out = jnp.einsum('bhqk,bhkd->bhqd', probs, vh)
            return out.transpose(0, 2, 1, 3).reshape(B, Sq, H)
        residual = hidden_states
        unet_size = residual.shape[1]
        end_pos = encoder_hidden_states.shape[1] - NUM_TOKENS
        enc = encoder_hidden_states[:, :end_pos, :]
        ca = encoder_hidden_states[:, end_pos:, :]
        query = hidden_states @ Wq
        keyt = enc @ Wk
        valt = enc @ Wv
        hs = _mha(query, keyt, valt)
        ca_q1 = jnp.einsum('btc,th->bch', ca, Wq_ca)
        indices = np.linspace(0, CROSS_ATTENTION_DIM - 1, unet_size).astype(np.int64)
        ca_q1 = ca_q1[:, indices, :]
        ca_hs1 = _mha(ca_q1, residual, residual)
        ca_q2 = ca_hs1 @ Wq
        ca_k2 = ca @ Wk_ca
        ca_v2 = ca @ Wv_ca
        ca_hs2 = _mha(ca_q2, ca_k2, ca_v2)
        out = hs + ca_hs2
        out = out @ Wout + b_out
        out = out + residual
        return out

    def _L1_xattn_ref(hidden_states, encoder_hidden_states, Wq, Wk, Wv, Wo, bo):
        import jax, jax.numpy as jnp
        import numpy as np
        HEADS = 20
        NUM_AOE = 16
        NUM_IP = 16
        B, Sq, H = hidden_states.shape
        Skv = encoder_hidden_states.shape[1]
        head_dim = H // HEADS
        residual = hidden_states
        q = (hidden_states @ Wq).reshape(B, Sq, HEADS, head_dim).transpose(0, 2, 1, 3)
        k = (encoder_hidden_states @ Wk).reshape(B, Skv, HEADS, head_dim).transpose(0, 2, 1, 3)
        v = (encoder_hidden_states @ Wv).reshape(B, Skv, HEADS, head_dim).transpose(0, 2, 1, 3)
        scores = jnp.einsum('bhqd,bhkd->bhqk', q, k) / jnp.sqrt(jnp.asarray(head_dim, q.dtype))
        probs = jax.nn.softmax(scores, axis=-1)
        scale_aoe = jnp.asarray(1.0, probs.dtype)
        scale_ip = jnp.asarray(1.0, probs.dtype)
        idx = jnp.arange(Skv)
        scale_vector = jnp.where(idx < NUM_AOE, scale_aoe, 1.0)
        scale_vector = jnp.where(idx >= Skv - NUM_IP, scale_vector * scale_ip, scale_vector)
        probs = probs * scale_vector
        probs = probs / probs.sum(axis=-1, keepdims=True)
        out = jnp.einsum('bhqk,bhkd->bhqd', probs, v)
        out = out.transpose(0, 2, 1, 3).reshape(B, Sq, H)
        out = out @ Wo + bo
        return out + residual
    x = _L0_xattn_ref(x, ctx_768, L0_xattn_Wq, L0_xattn_Wk, L0_xattn_Wv, L0_xattn_Wq_ca, L0_xattn_Wk_ca, L0_xattn_Wv_ca, L0_xattn_Wout, L0_xattn_b_out)
    x = _L1_xattn_ref(x, ctx_768, L1_xattn_Wq, L1_xattn_Wk, L1_xattn_Wv, L1_xattn_Wo, L1_xattn_bo)
    return x

_drawn_inputs = setup_inputs


def setup_inputs(seed=0):
    import zlib

    import numpy as np

    out = dict(_drawn_inputs(seed))
    spreads = {'L0_xattn_b_out': (0.0, 0.1), 'L1_xattn_bo': (0.0, 0.1)}
    factors = {'L0_xattn_Wq': 8.0,
     'L0_xattn_Wk': 8.0,
     'L0_xattn_Wq_ca': 30.842,
     'L0_xattn_Wk_ca': 8.0,
     'L1_xattn_Wq': 8.0,
     'L1_xattn_Wk': 8.0}
    for name, (base, spread) in spreads.items():
        noise = np.random.default_rng([zlib.crc32(name.encode()), seed]).standard_normal(out[name].shape)
        drawn = base * np.exp(spread * noise) if base else spread * noise
        out[name] = jnp.asarray(drawn.astype(out[name].dtype))
    for name, factor in factors.items():
        out[name] = (out[name] * factor).astype(out[name].dtype)
    return out
```

```python
from contextlib import ExitStack

import concourse.bass as bass
from concourse import mybir

F32 = mybir.dt.float32
F32R = mybir.dt.float32r
ALU = mybir.AluOpType
ACT = mybir.ActivationFunctionType
AX = mybir.AxisListType.X

B, SQ, HID = 16, 112, 320
SK, CAD, NTOK = 375, 192, 4
SKE = SK - NTOK
SKP = SK + 1
H0, D0 = 8, 40
H1, D1 = 20, 16
KC, NKC = 125, 3
P = 128
SCALE0 = float(D0) ** -0.5
SCALE1 = float(D1) ** -0.5

KV_COLS = 1344
W_K0, W_K1, W_V0, W_V1 = 0, 320, 704, 1024
C_KV = 0
C_WQ0 = 2 * KV_COLS
C_WQ1 = C_WQ0 + 3 * HID
C_WO1 = C_WQ1 + 3 * HID
C_WO0 = C_WO1 + 3 * HID
C_ALL = C_WO0 + 4 * HID
CUT = C_WQ1

UNITS = [
    (0, "K1_0", "c"), (1, "K1_1", "c"), (2, "K1_2", "c"), (3, "V1_0", "c"), (4, "W2", "n"), (4, "V1_1", "c"),
    (5, "V1_2", "c"), (6, "out1", "e"), (7, "q0", "n"), (8, "S2_0", "n"), (9, "S2_1", "n"), (11, "q0T_0", "n"),
    (12, "q0T_1", "n"), (13, "K0_0", "n"), (14, "K0_1", "n"), (15, "out0", "c"), (16, "K0_2", "n"),
    (17, "T2_0", "n"), (18, "x1T", "c"), (19, "T2_1", "n"), (20, "q1", "c"), (21, "PV2", "n"),
    (22, "q1T_0", "c"), (23, "q1T_1", "c"), (23, "V0_0", "n"), (24, "S3", "n"), (25, "q1T_2", "c"),
    (26, "V0_1", "n"), (27, "V0_2", "n"),
]
HEADS = H0 + H1
LAG_T, LAG_PV = 3, 4
O0_STEP, O1_STEP = H0 + LAG_PV, LAG_PV
K0_ROWS, K1_ROWS = 120, 128
DMAS_K0, DMAS_K1 = 9, 24
PSLOTS = 4
FIRST = 3
PER_TWO_UNITS, PER_TWO_HEADS = 2 * len(UNITS), 2 * HEADS


def groups_of(t):
    return (("n" if t < B - 1 else "") + ("c" if 0 <= t < B else "") + ("l" if 1 <= t <= B else "")
            + ("e" if t >= 2 else ""))


def steps_of(t):
    return ([*range(H0)] if "c" in groups_of(t) else []) + ([*range(H0, HEADS)] if "l" in groups_of(t) else [])


class Iteration:

    def __init__(self, t0, j=0):
        self.t0, self.j, self.t = t0, j, t0 + 2 * j
        self.groups = groups_of(t0)
        self.present = [(s, u) for s, u, g in UNITS if g in self.groups]
        before = sum(g in groups_of(t) for t in range(-1, t0) for _, _, g in UNITS)
        self.at = {u: before + i for i, (_, u) in enumerate(self.present)}
        self.head_at = {s: sum(len(steps_of(t)) for t in range(t0)) + i for i, s in enumerate(steps_of(t0))}
        self.before = Iteration(t0 - 1, j) if t0 >= 0 else None

    def of(self, step):
        return (self, step) if step >= 0 or self.before is None else (self.before, step + HEADS)

    def units(self, step):
        it, step = self.of(step)
        return [(it, u) for s, u in it.present if s == step]

    def head(self, step):
        it, step = self.of(step)
        return (it, step) if step in it.head_at else None

    def heads(self, step, more=0):
        return self.head_at[step] + 1 + more + PER_TWO_HEADS * self.j

    def batches(self, per, off, extra=0):
        return per * (self.t0 + off) + extra + 2 * per * self.j

    def bank(self, unit):
        return self.at[unit] % 2

    def filled(self, unit):
        return self.at[unit] + 1 + PER_TWO_UNITS * self.j

    def drained(self, unit):
        return self.at[unit] // 2 + 1 + len(UNITS) * self.j

    def parity(self, off):
        return (self.t0 + off) % 2

    def pairs(self, per, off):
        return per * ((self.t0 + off) // 2 + 1) + per * self.j


def xattn_kernel(nc, xT, xpad, ctxT, caS, caT, w_all, w_ca, wqT, bd96, consts, bias, out):
    scratch = nc.dram_tensor("v3_rows", [B * NTOK, H0 * 64], F32, kind="Internal").ap()

    with ExitStack() as ctx:
        def sb(name, shape, dt=F32):
            return ctx.enter_context(nc.sbuf_tensor(name, shape, dt))

        def pb(name, shape):
            return ctx.enter_context(nc.psum_tensor(name, shape, F32))

        def sem(name):
            return ctx.enter_context(nc.semaphore(name))

        WH = sb("WH", [P, C_ALL], F32R)
        WL = sb("WL", [P, C_ALL], F32R)
        arena = sb("arena", [P, 4416])
        stage = sb("stage", [P, 4, NKC, SKP])
        prob = arena[:, 0:PSLOTS * SKP].rearrange("p (s n) -> p s n", s=PSLOTS)
        probT = arena[:, 1504:2176].rearrange("p (s k q) -> p s k q", s=2, k=NKC)
        prob2 = arena[:, 2176:3072].rearrange("p (h k) -> p h k", h=H0)
        prob2T = arena[:, 3072:3968].rearrange("p (h q) -> p h q", h=H0)
        hs1T = arena[:, 3968:4416].rearrange("p (c q) -> p c q", c=4)
        k1_hi, k1_lo, k0_hi, k0_lo = (stage[:, i] for i in range(4))
        k0_stack = sb("k0_stack", [K0_ROWS, H0, SKP], F32R)
        k1_stack = [sb(f"k1_stack{i}", [K1_ROWS, H1 // 2, SKP], F32R) for i in range(2)]
        v0 = sb("v0", [P, NKC, H0 * 64])
        v1 = [sb(f"v1_{i}", [P, NKC, H1 * 32]) for i in range(2)]
        ctx_raw = sb("ctx_raw", [P, 2, SKP])
        ctx_hi = sb("ctx_hi", [P, 2, SKP], F32R)
        ctx_lo = sb("ctx_lo", [P, SKP], F32R)
        x_raw = sb("x_raw", [P, 3, SQ])
        x_hi = sb("x_hi", [P, 3, SQ], F32R)
        x_lo = sb("x_lo", [P, 2, SQ], F32R)
        qn = sb("qn", [SQ, H1 * 64], F32R)
        q0T = sb("q0T", [K0_ROWS, H0, SQ], F32R)
        q1T = [sb(f"q1T{i}", [P, H1 // 2, SQ], F32R) for i in range(2)]
        xp = sb("xp", [SQ, H0 * 64])
        act_hi = sb("act_hi", [P, 4, SQ], F32R)
        act_lo = sb("act_lo", [P, 4, SQ], F32R)
        x1 = sb("x1", [SQ, HID])
        x1b = [sb(f"x1b{i}", [SQ, HID]) for i in range(2)]
        xb = sb("xb", [SQ, HID])
        bias_sb = sb("bias_sb", [SQ, 2, HID])
        gq = sb("gq", [P, 4, B * 32])
        gb = sb("gb", [P, 4, 32])
        ca_raw = sb("ca_raw", [96, SQ])
        ca_st = sb("ca_st", [96, SQ], F32R)
        w2s = sb("w2s", [96, SQ], F32R)
        w2bd = sb("w2bd", [96, H0, SQ], F32R)
        bd = sb("bd", [P, 3, 96])
        cst = sb("cst", [P, 161])
        one = cst[:, 160:161]
        ident = cst[:, 0:128]
        mask96 = cst[0:96, 128:136]
        mask3 = cst[:, 136:160].rearrange("p (c h) -> p c h", c=3)
        caT_sb = gb[:, :, :].rearrange("p (a c) n -> p a (c n)", a=2)
        negmax = sb("negmax", [SQ, HEADS])
        psum_ = sb("psum_", [SQ, HEADS])
        rsum = sb("rsum", [SQ, HEADS])
        negmax2 = sb("negmax2", [SQ, H0])
        sum2 = sb("sum2", [SQ, H0])
        rsum2 = sb("rsum2", [SQ, H0])
        p3 = sb("p3", [SQ, H0, NTOK])
        negmax3 = sb("negmax3", [SQ, H0])
        sum3 = sb("sum3", [SQ, H0])
        rsum3 = sb("rsum3", [SQ, H0])
        outb = x1b

        bankS = [pb(f"bankS{i}", [P, 512]) for i in range(2)]
        bankT = [pb(f"bankT{i}", [P, 512]) for i in range(2)]
        bankO0 = pb("bankO0", [P, 512])
        bankO1 = pb("bankO1", [P, 512])
        bankX = [pb(f"bankX{i}", [P, 512]) for i in range(2)]
        O0 = bankO0[:, 0:4 * SQ].rearrange("p (c q) -> p c q", c=4)
        O1 = bankO1[:, 0:3 * SQ].rearrange("p (c q) -> p c q", c=3)

        w_loaded = sem("w_loaded")
        w2_loaded = sem("w2_loaded")
        w3_loaded = sem("w3_loaded")
        const_loaded = sem("const_loaded")
        w_rounded = sem("w_rounded")
        w_split = sem("w_split")
        zeroed = sem("zeroed")
        pro_pe = sem("pro_pe")
        pro_vec = sem("pro_vec")
        v3_stored = sem("v3_stored")
        x_loaded = sem("x_loaded")
        ca_loaded = sem("ca_loaded")
        ctx_loaded = sem("ctx_loaded")
        xp_loaded = sem("xp_loaded")
        v3_loaded = sem("v3_loaded")
        k0_stacked = sem("k0_stacked")
        k1_stacked = [sem(f"k1_stacked{i}") for i in range(2)]
        scores_done = sem("scores_done")
        max_done = sem("max_done")
        exp_done = sem("exp_done")
        rsum_done = sem("rsum_done")
        prob_ready = sem("prob_ready")
        probT_done = sem("probT_done")
        probT_copied = sem("probT_copied")
        pv_done = sem("pv_done")
        unit_filled = sem("unit_filled")
        bank_drained = [sem(f"bank_drained{i}") for i in range(2)]
        k1_rounded = sem("k1_rounded")
        k0_rounded = sem("k0_rounded")
        q0_rounded = sem("q0_rounded")
        q1_rounded = sem("q1_rounded")
        w2_rounded = sem("w2_rounded")
        x1T_rounded = sem("x1T_rounded")
        o0_rounded = sem("o0_rounded")
        o1_rounded = sem("o1_rounded")
        o0_split = sem("o0_split")
        o1_split = sem("o1_split")
        ca_split = sem("ca_split")
        w2_expanded = sem("w2_expanded")
        x_split = sem("x_split")
        ctx_split = sem("ctx_split")
        gb_copied = sem("gb_copied")
        xb_ready = sem("xb_ready")
        x1b_ready = sem("x1b_ready")
        max2_done = sem("max2_done")
        rsum2_done = sem("rsum2_done")
        prob2_ready = sem("prob2_ready")
        p3_vec = sem("p3_vec")
        exp3_done = sem("exp3_done")
        p3_ready = sem("p3_ready")
        out_stored = sem("out_stored")
        pool_chain = sem("pool_chain")

        def whole_run(eng, iteration):
            for t in range(-1, FIRST):
                iteration(Iteration(t))
            with eng.Fori(0, (B - 1 - FIRST) // 2) as j:
                iteration(Iteration(FIRST, j))
                iteration(Iteration(FIRST + 1, j))
            for t in range(B - 1, B + 2):
                iteration(Iteration(t))

        block = ctx.enter_context(nc.Block())

        @block.sync
        def _(sp):
            sp.dma_start(arena[:, 0:CUT], w_all[:, 0:CUT]).then_inc(w_loaded, 16)
            flat = stage[:, :, :, :].rearrange("p a c n -> p (a c n)")
            sp.dma_start(flat[:, 0:C_ALL - CUT], w_all[:, CUT:C_ALL]).then_inc(w2_loaded, 16)
            sp.dma_start(cst[:, :], consts).then_inc(const_loaded, 16)
            sp.dma_start(bd[:, :, :], bd96).then_inc(const_loaded, 16)
            sp.dma_start(caT_sb, caT).then_inc(const_loaded, 16)
            sp.dma_start(bias_sb[:, :, :], bias).then_inc(const_loaded, 16)
            sp.wait_ge(w_split, 1)
            sp.dma_start(arena[:, 0:1280], w_ca.rearrange("p a n -> p (a n)")).then_inc(w3_loaded, 16)
            sp.dma_start(arena[:, 1280:2816], wqT.rearrange("p a n -> p (a n)")).then_inc(w3_loaded, 16)
            sp.wait_ge(pro_vec, 2)
            sp.dma_start(scratch, v0[0:B * NTOK, 0, :]).then_inc(v3_stored, 16)

            xT_cols = xT.rearrange("b p c q -> p b (c q)")
            caS_cols = caS.rearrange("b p q -> p b q")
            xp_cols = xpad.rearrange("b p n -> p b n")
            ctx_cols = ctxT.rearrange("b p c n -> p b (c n)")

            def iteration(it):
                if "n" in it.groups:
                    n = it.t + 1
                    if "c" in it.groups:
                        sp.wait_ge(xb_ready, it.batches(1, 1))
                    sp.dma_start(x_raw[:, :, :].rearrange("p c q -> p (c q)").unsqueeze(1),
                                 xT_cols[:, bass.ds(n, 1), :]).then_inc(x_loaded, 16)
                    sp.dma_start(ca_raw[:, :].unsqueeze(1), caS_cols[:, bass.ds(n, 1), :]).then_inc(ca_loaded, 16)
                    sp.dma_start(xp[:, :].unsqueeze(1), xp_cols[:, bass.ds(n, 1), :]).then_inc(xp_loaded, 16)
                    sp.dma_start(ctx_raw[:, :, :].rearrange("p c n -> p (c n)").unsqueeze(1),
                                 ctx_cols[:, bass.ds(n, 1), :]).then_inc(ctx_loaded, 16)
                if "c" in it.groups:
                    dst = k1_stack[it.parity(0)]
                    sp.wait_ge(bank_drained[it.bank("K1_2")], it.drained("K1_2"))
                    for r in range(8):
                        nch = 3 if r < 4 else 2
                        for part, src in enumerate((k1_lo, k1_hi, k1_hi)):
                            to = 64 * (r % 2) + D1 * part
                            sp.dma_start(dst[to:to + D1, r // 2:r // 2 + 4 * (nch - 1) + 1:4, :].bitcast(F32),
                                         src[D1 * r:D1 * r + D1, 0:nch, :])\
                                .then_inc(k1_stacked[it.parity(0)], 16)
                if "n" in it.groups:
                    sp.wait_ge(bank_drained[it.bank("K0_2")], it.drained("K0_2"))
                    for r in range(3):
                        nch = 3 if r < 2 else 2
                        for part, src in enumerate((k0_lo, k0_hi, k0_hi)):
                            to = D0 * part
                            sp.dma_start(k0_stack[to:to + D0, r:r + 3 * (nch - 1) + 1:3, :].bitcast(F32),
                                         src[D0 * r:D0 * r + D0, 0:nch, :]).then_inc(k0_stacked, 16)
                    if "c" not in it.groups:
                        sp.wait_ge(v3_stored, 16)
                    sp.dma_start(v0[KC - NTOK:KC, NKC - 1, :], scratch[bass.ds(n * NTOK, NTOK), :])\
                        .then_inc(v3_loaded, 16)

            whole_run(sp, iteration)

        @block.gpsimd
        def _(pool):
            nc.gpsimd.memset(v0[:, :, :], 0.0).then_inc(zeroed, 1)
            for i in range(2):
                nc.gpsimd.memset(v1[i][:, :, :], 0.0).then_inc(zeroed, 1)
            nc.gpsimd.memset(qn[:, :].bitcast(F32), 0.0).then_inc(zeroed, 1)

            def rounded(hi, src):
                rows, cols = src.shape
                return nc.gpsimd.tensor_tensor(hi, src, one[0:rows, :].broadcast_to((rows, cols)), ALU.mult)

            def iteration(it):
                if "n" in it.groups:
                    if "c" not in it.groups:
                        pool.wait_ge(const_loaded, 64)
                    pool.wait_ge(ca_loaded, it.batches(16, 1, 16))
                    if "c" in it.groups:
                        pool.wait_ge(max2_done, it.batches(2, 1))
                    rounded(ca_st[:, :], ca_raw[:, :]).then_inc(pool_chain, 1)
                    pool.wait_ge(pool_chain, it.batches(5, 1, 1))
                    nc.gpsimd.tensor_tensor(ca_st[32:64, :], ca_raw[32:64, :], ca_st[32:64, :].bitcast(F32),
                                            ALU.subtract).then_inc(ca_split, 1)
                    pool.wait_ge(x_loaded, it.batches(16, 1, 16))
                    pool.wait_ge(ca_split, it.batches(1, 1, 1))
                    if "c" in it.groups:
                        pool.wait_ge(q0_rounded, it.batches(1, 1))
                    rounded(x_hi[:, :, :].rearrange("p c q -> p (c q)"),
                            x_raw[:, :, :].rearrange("p c q -> p (c q)")).then_inc(pool_chain, 1)
                    pool.wait_ge(pool_chain, it.batches(5, 1, 2))
                    nc.gpsimd.tensor_tensor(x_lo[:, :, :], x_raw[:, 0:2, :], x_hi[:, 0:2, :].bitcast(F32),
                                            ALU.subtract).then_inc(pool_chain, 1)
                    pool.wait_ge(pool_chain, it.batches(5, 1, 3))
                    nc.gpsimd.tensor_tensor(x_hi[64:128, 2, :], x_raw[64:128, 2, :],
                                            x_hi[64:128, 2, :].bitcast(F32), ALU.subtract).then_inc(x_split, 1)
                    pool.wait_ge(bank_drained[it.bank("W2")], it.drained("W2"))
                    pool.wait_ge(x_split, it.batches(1, 1, 1))
                    nc.gpsimd.tensor_tensor(
                        w2bd[:, :, :], w2s[:, :].bitcast(F32).unsqueeze(1).broadcast_to((96, H0, SQ)),
                        mask96.unsqueeze(2).broadcast_to((96, H0, SQ)), ALU.mult).then_inc(w2_expanded, 1)
                    pool.wait_ge(ctx_loaded, it.batches(16, 1, 16))
                    if "c" in it.groups:
                        pool.wait_ge(unit_filled, it.filled("V1_2"))
                    pool.wait_ge(w2_expanded, it.batches(1, 1, 1))
                    rounded(ctx_hi[:, :, :].rearrange("p c n -> p (c n)"),
                            ctx_raw[:, :, :].rearrange("p c n -> p (c n)")).then_inc(pool_chain, 1)
                    pool.wait_ge(pool_chain, it.batches(5, 1, 4))
                    nc.gpsimd.tensor_tensor(ctx_lo[:, :], ctx_raw[:, 0, :], ctx_hi[:, 0, :].bitcast(F32),
                                            ALU.subtract).then_inc(pool_chain, 1)
                    pool.wait_ge(pool_chain, it.batches(5, 1, 5))
                    nc.gpsimd.tensor_tensor(ctx_hi[64:128, 1, :], ctx_raw[64:128, 1, :],
                                            ctx_hi[64:128, 1, :].bitcast(F32), ALU.subtract).then_inc(ctx_split, 1)
                if "e" in it.groups:
                    pool.wait_ge(bank_drained[it.bank("out1")], it.drained("out1"))
                    pool.dma_start(out[bass.ds(it.t - 2, 1)].rearrange("a q n -> q (a n)"),
                                   outb[it.parity(-2)][:, :]).then_inc(out_stored, 16)
                if "n" in it.groups:
                    pool.wait_ge(rsum2_done, it.batches(1, 1, 1))
                    pool.wait_ge(ctx_split, it.batches(1, 1, 1))
                    nc.gpsimd.tensor_tensor(prob2[0:SQ], prob2[0:SQ],
                                            rsum2[:, :].unsqueeze(2).broadcast_to((SQ, H0, SQ)),
                                            ALU.mult).then_inc(prob2_ready, 1)
                if "c" in it.groups:
                    pool.wait_ge(bank_drained[it.bank("out0")], it.drained("out0"))
                    if it.t0 >= 2:
                        pool.wait_ge(out_stored, it.batches(16, -1))
                    if "n" in it.groups:
                        pool.wait_ge(prob2_ready, it.batches(1, 1, 1))
                    nc.gpsimd.tensor_tensor(x1b[it.parity(0)][:, :], x1[:, :], bias_sb[:, 1, :], ALU.add)\
                        .then_inc(x1b_ready, 1)
                if "n" in it.groups:
                    pool.wait_ge(xp_loaded, it.batches(16, 1, 16))
                    pool.wait_ge(unit_filled, it.filled("PV2"))
                    if "c" in it.groups:
                        pool.wait_ge(x1b_ready, it.batches(1, 0, 1))
                    nc.gpsimd.tensor_tensor(
                        xb[:, :].rearrange("p (h d) -> p h d", h=H0),
                        xp[:, :].rearrange("p (h d) -> p h d", h=H0)[:, :, 0:D0],
                        bias_sb[:, 0, :].rearrange("p (h d) -> p h d", h=H0), ALU.add).then_inc(xb_ready, 1)
            whole_run(pool, iteration)
            pool.wait_ge(out_stored, 16 * B)

        @block.scalar
        def _(act):
            act.wait_ge(w_loaded, 16)
            nc.scalar.activation(WH[:, 0:CUT], arena[:, 0:CUT], ACT.Copy).then_inc(w_rounded, 1)
            act.wait_ge(w2_loaded, 16)
            flat = stage[:, :, :, :].rearrange("p a c n -> p (a c n)")
            nc.scalar.activation(WH[:, CUT:C_ALL], flat[:, 0:C_ALL - CUT], ACT.Copy).then_inc(w_rounded, 1)

            def exps2(it, half):
                act.wait_ge(max2_done, it.batches(2, 1, half + 1))
                X = bankX[it.bank(f"S2_{half}")]
                for h in range(4 * half, 4 * half + 4):
                    last = nc.scalar.activation(prob2[0:SQ, h, :], X[0:SQ, (h % 4) * SQ:(h % 4 + 1) * SQ], ACT.Exp,
                                                bias=negmax2[:, h:h + 1], accum_out=sum2[:, h:h + 1])
                last.then_inc(bank_drained[it.bank(f"S2_{half}")], 1)

            def unit(it, u):
                X = bankX[it.bank(u)]
                free = bank_drained[it.bank(u)]
                kind, _, i = u.partition("_")
                i = int(i or 0)
                if kind in ("S2", "S3", "out0", "out1"):
                    return
                act.wait_ge(unit_filled, it.filled(u))
                if kind == "K1":
                    if i == 0 and it.t0 >= 1:
                        act.wait_ge(k1_stacked[it.parity(-1)], it.pairs(16 * DMAS_K1, -1))
                    if i == 0 and it.t0 == 0:
                        act.wait_ge(w_split, 2)
                    rows = P if i < 2 else 64
                    nc.scalar.activation(k1_hi[0:rows, i, :].bitcast(F32R), X[0:rows, 0:SKP], ACT.Copy)\
                        .then_inc(k1_rounded, 1)
                elif kind == "K0":
                    if i == 0 and it.t0 >= 0:
                        act.wait_ge(k0_stacked, it.batches(16 * DMAS_K0, 1))
                    if i == 0 and it.t0 < 0:
                        act.wait_ge(w_split, 2)
                    rows = 120 if i < 2 else 80
                    nc.scalar.activation(k0_hi[0:rows, i, :].bitcast(F32R), X[0:rows, 0:SKP], ACT.Copy)\
                        .then_inc(k0_rounded, 1)
                elif kind == "V0":
                    rows = KC if i < 2 else KC - NTOK
                    if it.t0 < 0:
                        act.wait_ge(v3_stored, 16)
                    nc.scalar.activation(v0[0:rows, i, :].rearrange("p (h d) -> p h d", h=H0)[:, :, 0:D0],
                                         X[0:rows, 0:HID].rearrange("p (h d) -> p h d", h=H0), ACT.Copy)\
                        .then_inc(free, 1)
                elif kind == "V1":
                    if i == 0 and "e" in it.groups:
                        act.wait_ge(pv_done, it.before.heads(HEADS - 1))
                    dst = v1[it.parity(0)][0:KC, i, :].rearrange("p (g a d) -> p g a d", a=4, d=D1)
                    src = X[0:KC, 0:HID].rearrange("p (g a d) -> p g a d", a=2, d=D1)
                    nc.scalar.activation(dst[:, :, 0, :], src[:, :, 0, :], ACT.Copy)
                    nc.scalar.activation(dst[:, :, 3, :], src[:, :, 1, :], ACT.Copy).then_inc(free, 1)
                elif kind == "q0":
                    dst = qn[:, 0:H0 * 120].rearrange("p (h a d) -> p h a d", h=H0, a=3)[:, :, 0:3:2, :]
                    src = X[0:SQ, 0:HID].rearrange("p (h d) -> p h d", h=H0).unsqueeze(2)
                    nc.scalar.activation(dst, src.broadcast_to((SQ, H0, 2, D0)), ACT.Copy, scale=SCALE0)\
                        .then_inc(q0_rounded, 1)
                elif kind == "q1":
                    dst = qn[:, :].rearrange("p (h a d) -> p h a d", h=H1, a=4)[:, :, 0:3:2, :]
                    src = X[0:SQ, 0:HID].rearrange("p (h d) -> p h d", h=H1).unsqueeze(2)
                    nc.scalar.activation(dst, src.broadcast_to((SQ, H1, 2, D1)), ACT.Copy, scale=SCALE1)\
                        .then_inc(q1_rounded, 1)
                elif kind == "q0T":
                    if it.t0 < 0 and i == 0:
                        act.wait_ge(pro_vec, 6)
                    nc.scalar.activation(q0T[:, 4 * i:4 * i + 4, :].rearrange("p h q -> p (h q)"),
                                         X[0:K0_ROWS, 0:4 * SQ], ACT.Copy).then_inc(free, 1)
                    if i == 0:
                        nc.scalar.activation(gb[:, :, :], gq[:, :, bass.ds((it.t + 1) * 32, 32)], ACT.Copy)\
                            .then_inc(gb_copied, 1)
                elif kind == "q1T":
                    g = 4 if i < 2 else 2
                    nc.scalar.activation(q1T[it.parity(0)][:, 4 * i:4 * i + g, :].rearrange("p h q -> p (h q)"),
                                         X[:, 0:g * SQ], ACT.Copy).then_inc(free, 1)
                elif kind == "W2":
                    nc.scalar.activation(w2s[:, :], X[0:96, 0:SQ], ACT.Copy, scale=SCALE0).then_inc(w2_rounded, 1)
                elif kind == "T2":
                    nc.scalar.activation(prob2T[0:SQ, 4 * i:4 * i + 4, :].rearrange("p h q -> p (h q)"),
                                         X[0:SQ, 0:4 * SQ], ACT.Copy).then_inc(free, 1)
                elif kind == "PV2":
                    nc.scalar.activation(hs1T.rearrange("p c q -> p (c q)"), X[:, 0:4 * SQ], ACT.Copy)\
                        .then_inc(free, 1)
                elif kind == "x1T":
                    nc.scalar.activation(act_hi[:, 0:2, :].rearrange("p c q -> p (c q)"), X[:, 0:2 * SQ], ACT.Copy)
                    nc.scalar.activation(act_hi[0:64, 2, :], X[0:64, 2 * SQ:3 * SQ], ACT.Copy)\
                        .then_inc(x1T_rounded, 1)

            def iteration(it):
                for s in range(HEADS):
                    if s == O0_STEP and "c" in it.groups:
                        act.wait_ge(pv_done, it.heads(H0 - 1))
                        nc.scalar.activation(act_hi[:, :, :].rearrange("p c q -> p (c q)"), bankO0[:, 0:4 * SQ],
                                             ACT.Copy).then_inc(o0_rounded, 1)
                    if s == O1_STEP and "e" in it.groups:
                        act.wait_ge(pv_done, it.before.heads(HEADS - 1))
                        nc.scalar.activation(act_hi[:, 0:2, :].rearrange("p c q -> p (c q)"),
                                             bankO1[:, 0:2 * SQ], ACT.Copy)
                        nc.scalar.activation(act_hi[0:64, 2, :], bankO1[0:64, 2 * SQ:3 * SQ], ACT.Copy)\
                            .then_inc(o1_rounded, 1)
                    for at, u in it.units(s - 1):
                        unit(at, u)
                    for at, u in it.units(s - 2):
                        if u == "S2_0":
                            exps2(at, 0)
                        elif u == "S2_1":
                            exps2(at, 1)
                        elif u == "S3":
                            act.wait_ge(bank_drained[at.bank("S3")], at.drained("S3"))
                            nc.scalar.activation(p3[:, :, :], p3[:, :, :], ACT.Exp).then_inc(exp3_done, 1)
                    if it.head(s - LAG_T):
                        at, h = it.head(s - LAG_T)
                        act.wait_ge(probT_done, at.heads(h))
                        if at.head_at[h] >= 2:
                            act.wait_ge(pv_done, at.heads(h, -2))
                        nc.scalar.activation(probT[0:KC, h % 2], bankT[h % 2][0:KC, 0:NKC * SQ]
                                             .rearrange("p (k q) -> p k q", k=NKC), ACT.Copy)\
                            .then_inc(probT_copied, 1)
                    if it.head(s):
                        act.wait_ge(max_done, it.heads(s))
                        keys = SKE if s < H0 else SK
                        nc.scalar.activation(prob[0:SQ, s % PSLOTS, 0:keys], bankS[s % 2][0:SQ, 0:keys], ACT.Exp,
                                             bias=negmax[:, s:s + 1], accum_out=psum_[:, s:s + 1])\
                            .then_inc(exp_done, 1)

            whole_run(act, iteration)

        @block.vector
        def _(dve):
            dve.wait_ge(w_rounded, 1)
            nc.vector.tensor_tensor(WL[:, 0:CUT], arena[:, 0:CUT], WH[:, 0:CUT].bitcast(F32), ALU.subtract)\
                .then_inc(w_split, 1)
            flat = stage[:, :, :, :].rearrange("p a c n -> p (a c n)")
            dve.wait_ge(w_rounded, 2)
            nc.vector.tensor_tensor(WL[:, CUT:C_ALL], flat[:, 0:C_ALL - CUT], WH[:, CUT:C_ALL].bitcast(F32),
                                    ALU.subtract).then_inc(w_split, 1)
            dve.wait_ge(zeroed, 4)
            dve.wait_ge(pro_pe, 1)
            k2bd = arena[:, 2816:4352].rearrange("p (c b h k) -> p c b h k", c=3, b=B, h=H0)
            for c in range(3):
                rows = P if c < 2 else 64
                last = nc.vector.tensor_tensor(
                    k2bd[0:rows, c],
                    bankT[0][0:rows, c * 64:c * 64 + 64].rearrange("p (b k) -> p b k", b=B)
                    .unsqueeze(2).broadcast_to((rows, B, H0, NTOK)),
                    mask3[0:rows, c, :].unsqueeze(1).unsqueeze(3).broadcast_to((rows, B, H0, NTOK)), ALU.mult)
            last.then_inc(pro_vec, 1)
            dve.wait_ge(pro_pe, 2)
            nc.vector.tensor_copy(v0[0:B * NTOK, 0, :].rearrange("p (h d) -> p h d", h=H0)[:, :, 0:D0],
                                  bankT[1][0:B * NTOK, 0:HID].rearrange("p (h d) -> p h d", h=H0))\
                .then_inc(pro_vec, 1)
            banks = [bankS[0], bankS[1], bankO0, bankO1]
            for m in range(4):
                dve.wait_ge(pro_pe, 3 + m)
                nc.vector.tensor_scalar(gq[:, m, :], banks[m][:, :], SCALE0, None, ALU.mult).then_inc(pro_vec, 1)

            def scaled_lo(dst, src, scale, hi):
                return nc.vector.scalar_tensor_tensor(out=dst, in0=src, scalar=scale, in1=hi, op0=ALU.mult,
                                                      op1=ALU.subtract)

            def unit(it, u):
                X = bankX[it.bank(u)]
                free = bank_drained[it.bank(u)]
                kind, _, i = u.partition("_")
                i = int(i or 0)
                if kind == "K1":
                    dve.wait_ge(k1_rounded, it.batches(3, 0, i + 1))
                    rows = P if i < 2 else 64
                    nc.vector.tensor_tensor(k1_lo[0:rows, i, :].bitcast(F32R), X[0:rows, 0:SKP],
                                            k1_hi[0:rows, i, :], ALU.subtract).then_inc(free, 1)
                elif kind == "K0":
                    dve.wait_ge(k0_rounded, it.batches(3, 1, i + 1))
                    rows = 120 if i < 2 else 80
                    nc.vector.tensor_tensor(k0_lo[0:rows, i, :].bitcast(F32R), X[0:rows, 0:SKP],
                                            k0_hi[0:rows, i, :], ALU.subtract).then_inc(free, 1)
                elif kind == "q0":
                    dve.wait_ge(q0_rounded, it.batches(1, 1, 1))
                    parts = qn[:, 0:H0 * 120].rearrange("p (h a d) -> p h a d", h=H0, a=3)
                    scaled_lo(parts[:, :, 1, :], X[0:SQ, 0:HID].rearrange("p (h d) -> p h d", h=H0), SCALE0,
                              parts[:, :, 0, :].bitcast(F32)).then_inc(free, 1)
                elif kind == "q1":
                    dve.wait_ge(q1_rounded, it.batches(1, 0, 1))
                    parts = qn[:, :].rearrange("p (h a d) -> p h a d", h=H1, a=4)
                    scaled_lo(parts[:, :, 1, :], X[0:SQ, 0:HID].rearrange("p (h d) -> p h d", h=H1), SCALE1,
                              parts[:, :, 0, :].bitcast(F32)).then_inc(free, 1)
                elif kind == "W2":
                    dve.wait_ge(w2_rounded, it.batches(1, 1, 1))
                    scaled_lo(w2s[64:96, :], X[64:96, 0:SQ], SCALE0, w2s[64:96, :].bitcast(F32)).then_inc(free, 1)
                elif kind == "S2":
                    dve.wait_ge(unit_filled, it.filled(u))
                    nc.vector.tensor_reduce(negmax2[:, 4 * i:4 * i + 4],
                                            X[0:SQ, 0:4 * SQ].rearrange("p (h k) -> p h k", h=4), axis=AX,
                                            op=ALU.max, negate=True).then_inc(max2_done, 1)
                elif kind == "S3":
                    dve.wait_ge(unit_filled, it.filled(u))
                    sc = X[0:SQ, 0:H0 * NTOK].rearrange("p (h k) -> p h k", h=H0)
                    nc.vector.tensor_reduce(negmax3[:, :], sc, axis=AX, op=ALU.max, negate=True)\
                        .then_inc(p3_vec, 1)
                    dve.wait_ge(p3_vec, it.batches(3, 1, 1))
                    nc.vector.tensor_tensor(p3[:, :, :], sc,
                                            negmax3[:, :].unsqueeze(2).broadcast_to((SQ, H0, NTOK)), ALU.add)\
                        .then_inc(free, 1)
                elif kind == "out0":
                    dve.wait_ge(unit_filled, it.filled(u))
                    dve.wait_ge(xb_ready, it.batches(1, 0, 1))
                    if it.t0 >= 1:
                        dve.wait_ge(x1b_ready, it.batches(1, 0))
                    nc.vector.tensor_tensor(x1[:, :], X[0:SQ, 0:HID], xb[:, :], ALU.add).then_inc(free, 1)
                elif kind == "x1T":
                    dve.wait_ge(x1T_rounded, it.batches(1, 0, 1))
                    nc.vector.tensor_tensor(act_lo[:, 0:2, :].rearrange("p c q -> p (c q)"), X[:, 0:2 * SQ],
                                            act_hi[:, 0:2, :].rearrange("p c q -> p (c q)").bitcast(F32),
                                            ALU.subtract)
                    nc.vector.tensor_tensor(act_hi[64:128, 2, :], X[0:64, 2 * SQ:3 * SQ],
                                            act_hi[0:64, 2, :].bitcast(F32), ALU.subtract).then_inc(free, 1)
                elif kind == "out1":
                    dve.wait_ge(unit_filled, it.filled(u))
                    y = x1b[it.parity(-2)]
                    dve.wait_ge(x1b_ready, it.batches(1, -2, 1))
                    nc.vector.tensor_tensor(y[:, :], X[0:SQ, 0:HID], y[:, :], ALU.add).then_inc(free, 1)

            def iteration(it):
                for s in range(HEADS):
                    if it.head(s):
                        dve.wait_ge(scores_done, it.heads(s))
                        keys = SKE if s < H0 else SK
                        nc.vector.tensor_reduce(negmax[:, s:s + 1], bankS[s % 2][0:SQ, 0:keys], axis=AX, op=ALU.max,
                                                negate=True).then_inc(max_done, 1)
                    if it.head(s - 1):
                        at, h = it.head(s - 1)
                        dve.wait_ge(exp_done, at.heads(h))
                        nc.vector.reciprocal(rsum[:, h:h + 1], psum_[:, h:h + 1]).then_inc(rsum_done, 1)
                    if s == O0_STEP and "c" in it.groups:
                        dve.wait_ge(o0_rounded, it.batches(1, 0, 1))
                        nc.vector.tensor_tensor(act_lo[:, :, :].rearrange("p c q -> p (c q)"), bankO0[:, 0:4 * SQ],
                                                act_hi[:, :, :].rearrange("p c q -> p (c q)").bitcast(F32),
                                                ALU.subtract).then_inc(o0_split, 1)
                    if s == O1_STEP and "e" in it.groups:
                        dve.wait_ge(o1_rounded, it.batches(1, -2, 1))
                        nc.vector.tensor_tensor(act_lo[:, 0:2, :].rearrange("p c q -> p (c q)"),
                                                bankO1[:, 0:2 * SQ],
                                                act_hi[:, 0:2, :].rearrange("p c q -> p (c q)").bitcast(F32),
                                                ALU.subtract)
                        nc.vector.tensor_tensor(act_hi[64:128, 2, :], bankO1[0:64, 2 * SQ:3 * SQ],
                                                act_hi[0:64, 2, :].bitcast(F32), ALU.subtract).then_inc(o1_split, 1)
                    for at, u in it.units(s - 1):
                        unit(at, u)
                    for at, u in it.units(s - 3):
                        if u == "S2_1":
                            dve.wait_ge(bank_drained[at.bank("S2_0")], at.drained("S2_0"))
                            dve.wait_ge(bank_drained[at.bank("S2_1")], at.drained("S2_1"))
                            nc.vector.reciprocal(rsum2[:, :], sum2[:, :]).then_inc(rsum2_done, 1)
                        if u == "S3":
                            dve.wait_ge(exp3_done, at.batches(1, 1, 1))
                            nc.vector.reduce_sum(sum3[:, :], p3[:, :, :], axis=AX).then_inc(p3_vec, 1)
                            dve.wait_ge(p3_vec, at.batches(3, 1, 2))
                            nc.vector.reciprocal(rsum3[:, :], sum3[:, :]).then_inc(p3_vec, 1)
                            dve.wait_ge(p3_vec, at.batches(3, 1, 3))
                            nc.vector.tensor_tensor(p3[:, :, :], p3[:, :, :],
                                                    rsum3[:, :].unsqueeze(2).broadcast_to((SQ, H0, NTOK)), ALU.mult)\
                                .then_inc(p3_ready, 1)
                    if it.head(s - 1):
                        at, h = it.head(s - 1)
                        keys = SKE if h < H0 else SK
                        slot = prob[0:SQ, h % PSLOTS, :]
                        if h < H0:
                            if h == 0:
                                dve.wait_ge(p3_ready, at.batches(1, 0, 1))
                            if at.head_at[h] >= PSLOTS:
                                dve.wait_ge(probT_done, at.heads(h, -PSLOTS))
                            nc.vector.tensor_copy(slot[:, SKE:SK], p3[:, h, :])
                        dve.wait_ge(rsum_done, at.heads(h))
                        nc.vector.tensor_scalar(slot[:, 0:keys], slot[:, 0:keys], rsum[:, h:h + 1], None,
                                                ALU.mult).then_inc(prob_ready, 1)

            whole_run(dve, iteration)

        @block.tensor
        def _(pe):
            pe.wait_ge(const_loaded, 64)
            pe.wait_ge(w3_loaded, 32)
            wca = arena[:, 0:1280].rearrange("p (a n) -> p a n", a=2)
            wqT_sb = arena[:, 1280:2816].rearrange("p (c n) -> p c n", c=3)
            for c in range(3):
                m = P if c < 2 else 64
                for a in range(2):
                    k = P if a == 0 else 64
                    last = nc.tensor.matmul(bankT[0][0:m, c * 64:c * 64 + 64], wca[0:k, a, c * P:c * P + m],
                                            caT_sb[0:k, a, :], start=(a == 0), stop=(a == 1))
            last.then_inc(pro_pe, 1)
            for a in range(2):
                k = P if a == 0 else 64
                last = nc.tensor.matmul(bankT[1][0:64, 0:HID], caT_sb[0:k, a, :], wca[0:k, a, HID:2 * HID],
                                        start=(a == 0), stop=(a == 1))
            last.then_inc(pro_pe, 1)
            pe.wait_ge(pro_vec, 1)
            k2bd = arena[:, 2816:4352].rearrange("p (c n) -> p c n", c=3)
            banks = [bankS[0], bankS[1], bankO0, bankO1]
            for m in range(4):
                for c in range(3):
                    k = P if c < 2 else 64
                    last = nc.tensor.matmul(banks[m][:, :], wqT_sb[0:k, c, m * P:m * P + P], k2bd[0:k, c, :],
                                            start=(c == 0), stop=(c == 2))
                last.then_inc(pro_pe, 1)
            pe.wait_ge(pro_vec, 6)
            pe.wait_ge(w_split, 2)

            def in_parts(dst, passes):
                for n, (lhs, rhs) in enumerate(passes):
                    last = nc.tensor.matmul(dst, lhs, rhs, start=(n == 0), stop=(n == len(passes) - 1))
                return last

            def unit(it, u):
                X = bankX[it.bank(u)]
                kind, _, i = u.partition("_")
                i = int(i or 0)
                if it.t0 > -1 or it.at[u] >= 2:
                    pe.wait_ge(bank_drained[it.bank(u)], it.drained(u) - 1)
                if kind in ("K0", "K1"):
                    if i == 0 and kind == "K0":
                        pe.wait_ge(ctx_split, it.batches(1, 1, 1))
                    lo, m = (W_K1 + P * i, P) if kind == "K1" else (W_K0 + 120 * i, 120 if i < 2 else 80)
                    a, b = slice(lo, lo + m), slice(KV_COLS + lo, KV_COLS + lo + m)
                    last = in_parts(X[0:m, 0:SKP], [
                        (WH[:, a], ctx_hi[:, 0, :]), (WH[:, a], ctx_lo[:, :]), (WL[:, a], ctx_hi[:, 0, :]),
                        (WH[:, b], ctx_hi[:, 1, :]), (WL[:, b], ctx_hi[:, 1, :])])
                elif kind in ("V0", "V1"):
                    lo = W_V0 if kind == "V0" else W_V1
                    a, b = slice(lo, lo + HID), slice(KV_COLS + lo, KV_COLS + lo + HID)
                    k = slice(KC * i, KC * i + KC)
                    last = in_parts(X[0:KC, 0:HID], [
                        (ctx_hi[:, 0, k], WH[:, a]), (ctx_lo[:, k], WH[:, a]), (ctx_hi[:, 0, k], WL[:, a]),
                        (ctx_hi[:, 1, k], WH[:, b]), (ctx_hi[:, 1, k], WL[:, b])])
                elif kind in ("q0", "q1", "out1"):
                    if kind == "q0":
                        pe.wait_ge(x_split, it.batches(1, 1, 1))
                        hi, lo, w = x_hi, x_lo, C_WQ0
                    elif kind == "q1":
                        pe.wait_ge(bank_drained[it.bank("x1T")], it.drained("x1T"))
                        hi, lo, w = act_hi, act_lo, C_WQ1
                    else:
                        pe.wait_ge(o1_split, it.batches(1, -2, 1))
                        hi, lo, w = act_hi, act_lo, C_WO1
                    w0, w1, w2 = (slice(w + HID * c, w + HID * c + HID) for c in range(3))
                    last = in_parts(X[0:SQ, 0:HID], [
                        (hi[:, 0, :], WH[:, w0]), (hi[:, 0, :], WL[:, w0]), (lo[:, 0, :], WH[:, w0]),
                        (hi[:, 1, :], WH[:, w1]), (hi[:, 1, :], WL[:, w1]), (lo[:, 1, :], WH[:, w1]),
                        (hi[:, 2, :], WH[:, w2]), (hi[:, 2, :], WL[:, w2])])
                elif kind == "out0":
                    pe.wait_ge(o0_split, it.batches(1, 0, 1))
                    passes = []
                    for c in range(4):
                        w = slice(C_WO0 + HID * c, C_WO0 + HID * c + HID)
                        passes += [(act_hi[:, c, :], WH[:, w]), (act_hi[:, c, :], WL[:, w]),
                                   (act_lo[:, c, :], WH[:, w])]
                    last = in_parts(X[0:SQ, 0:HID], passes)
                elif kind == "q0T":
                    if i == 0:
                        pe.wait_ge(bank_drained[it.bank("q0")], it.drained("q0"))
                    for h in range(4):
                        c = 120 * (4 * i + h)
                        last = nc.tensor.transpose(X[0:K0_ROWS, h * SQ:h * SQ + SQ],
                                                   qn[:, c:c + 120].bitcast(F32), ident[0:SQ, 0:SQ])
                elif kind == "q1T":
                    if i == 0:
                        pe.wait_ge(bank_drained[it.bank("q1")], it.drained("q1"))
                    for g in range(4 if i < 2 else 2):
                        c = 128 * (4 * i + g)
                        last = nc.tensor.transpose(X[:, g * SQ:g * SQ + SQ],
                                                   qn[:, c:c + 128].bitcast(F32), ident[0:SQ, 0:SQ])
                elif kind == "x1T":
                    pe.wait_ge(bank_drained[it.bank("out0")], it.drained("out0"))
                    for c in range(3):
                        m = P if c < 2 else 64
                        last = nc.tensor.transpose(X[0:m, c * SQ:c * SQ + SQ], x1[:, c * P:c * P + m],
                                                   ident[0:SQ, 0:SQ])
                elif kind == "W2":
                    pe.wait_ge(x_loaded, it.batches(16, 1, 16))
                    for c in range(3):
                        k = P if c < 2 else 64
                        last = nc.tensor.matmul(X[0:96, 0:SQ], bd[0:k, c, :], x_raw[0:k, c, :],
                                                start=(c == 0), stop=(c == 2))
                elif kind == "S2":
                    if i == 0:
                        pe.wait_ge(ca_split, it.batches(1, 1, 1))
                        pe.wait_ge(w2_expanded, it.batches(1, 1, 1))
                    last = nc.tensor.matmul(X[0:SQ, 0:4 * SQ], ca_st[:, :],
                                            w2bd[:, 4 * i:4 * i + 4, :].rearrange("p h q -> p (h q)"),
                                            start=True, stop=True)
                elif kind == "T2":
                    if i == 0:
                        pe.wait_ge(prob2_ready, it.batches(1, 1, 1))
                    for h in range(4):
                        last = nc.tensor.transpose(X[0:SQ, h * SQ:h * SQ + SQ], prob2[0:SQ, 4 * i + h, :],
                                                   ident[0:SQ, 0:SQ])
                elif kind == "PV2":
                    pe.wait_ge(xp_loaded, it.batches(16, 1, 16))
                    pe.wait_ge(bank_drained[it.bank("T2_0")], it.drained("T2_0"))
                    pe.wait_ge(bank_drained[it.bank("T2_1")], it.drained("T2_1"))
                    for h in range(H0):
                        last = nc.tensor.matmul(X[64 * (h % 2):64 * (h % 2) + 64, (h // 2) * SQ:(h // 2 + 1) * SQ],
                                                xp[:, 64 * h:64 * h + 64], prob2T[0:SQ, h, :],
                                                start=True, stop=True)
                elif kind == "S3":
                    pe.wait_ge(bank_drained[it.bank("PV2")], it.drained("PV2"))
                    pe.wait_ge(gb_copied, it.batches(1, 1, 1))
                    for c in range(4):
                        last = nc.tensor.matmul(X[0:SQ, 0:32], hs1T[:, c, :], gb[:, c, :], start=(c == 0),
                                                stop=(c == 3))
                last.then_inc(unit_filled, 1)

            def scores(it, s):
                if it.head_at[s] >= 2:
                    pe.wait_ge(exp_done, it.heads(s, -2))
                if s < H0:
                    if s == 0:
                        pe.wait_ge(k0_stacked, it.batches(16 * DMAS_K0, 0, 16 * DMAS_K0))
                    nc.tensor.matmul(bankS[s % 2][0:SQ, 0:SKE + 1], q0T[:, s, :], k0_stack[:, s, 0:SKE + 1],
                                     start=True, stop=True).then_inc(scores_done, 1)
                else:
                    h, par = s - H0, it.parity(-1)
                    if h == 0:
                        pe.wait_ge(k1_stacked[par], it.pairs(16 * DMAS_K1, -1))
                    row = slice(64 * (h % 2), 64 * (h % 2) + 3 * D1)
                    nc.tensor.matmul(bankS[s % 2][0:SQ, 0:SKP], q1T[par][row, h // 2, :],
                                     k1_stack[par][row, h // 2, :], start=True, stop=True)\
                        .then_inc(scores_done, 1)

            def transposes(it, s):
                pe.wait_ge(prob_ready, it.heads(s))
                if it.head_at[s] >= 2:
                    pe.wait_ge(probT_copied, it.heads(s, -2))
                for k in range(NKC):
                    last = nc.tensor.transpose(bankT[s % 2][0:KC, k * SQ:(k + 1) * SQ],
                                               prob[0:SQ, s % PSLOTS, KC * k:KC * k + KC], ident[0:SQ, 0:SQ])
                last.then_inc(probT_done, 1)

            def attend(it, s):
                pe.wait_ge(probT_copied, it.heads(s))
                if s < H0:
                    if s == 0:
                        pe.wait_ge(v3_loaded, it.batches(16, 0, 16))
                        if it.t0 >= 1:
                            pe.wait_ge(o0_split, it.batches(1, 0))
                    dst, c = bankO0[64 * (s % 2):64 * (s % 2) + 64, (s // 2) * SQ:(s // 2 + 1) * SQ], 64 * s
                    for k in range(NKC):
                        last = nc.tensor.matmul(dst, v0[0:KC, k, c:c + 64], probT[0:KC, s % 2, k, :],
                                                start=(k == 0), stop=(k == NKC - 1))
                else:
                    h = s - H0
                    g = h // 2
                    if h == 0 and it.t0 >= 2:
                        pe.wait_ge(o1_split, it.batches(1, -1))
                    dst = bankO1[32 * (g % 4):32 * (g % 4) + 32, (g // 4) * SQ:(g // 4 + 1) * SQ]
                    for k in range(NKC):
                        last = nc.tensor.matmul(dst, v1[it.parity(-1)][0:KC, k, 32 * h:32 * h + 32],
                                                probT[0:KC, s % 2, k, :], start=(h % 2 == 0 and k == 0),
                                                stop=(h % 2 == 1 and k == NKC - 1))
                last.then_inc(pv_done, 1)

            def iteration(it):
                for s in range(HEADS):
                    if it.head(s):
                        scores(it, s)
                    if it.head(s - LAG_T):
                        transposes(*it.head(s - LAG_T))
                    if it.head(s - LAG_PV):
                        attend(*it.head(s - LAG_PV))
                    for at, u in it.units(s):
                        unit(at, u)

            whole_run(pe, iteration)


def kernel(x, ctx_768, L0_xattn_Wq, L0_xattn_Wk, L0_xattn_Wv, L0_xattn_Wq_ca, L0_xattn_Wk_ca, L0_xattn_Wv_ca,
           L0_xattn_Wout, L0_xattn_b_out, L1_xattn_Wq, L1_xattn_Wk, L1_xattn_Wv, L1_xattn_Wo, L1_xattn_bo):
    import numpy as np
    import concourse.bacc as bacc
    from concourse.bass_utils import run_bass_kernel_spmd

    f = np.float32

    def rows3(w):
        return np.stack([w[..., 0:128, :], w[..., 128:256, :],
                         np.concatenate([w[..., 256:320, :]] * 2, axis=-2)], axis=-2)

    def head_rows(w):
        p = np.zeros((H0, 64) + w.shape[1:], f)
        p[:, 0:D0] = w.reshape((H0, D0) + w.shape[1:])
        return p.reshape((4, 128) + w.shape[1:]).transpose(1, 0, 2)

    x, ctx_768 = np.asarray(x), np.asarray(ctx_768)
    xT = np.ascontiguousarray(rows3(x.transpose(0, 2, 1)).reshape(B, 128, 3, SQ))
    xpad = np.zeros((B, SQ, H0, 64), f)
    xpad[..., 0:D0] = x.reshape(B, SQ, H0, D0)
    xpad = xpad.reshape(B, SQ, H0 * 64)
    cT = np.zeros((B, CAD, SKP), f)
    cT[:, :, 0:SK] = ctx_768.transpose(0, 2, 1)
    ctxT = np.ascontiguousarray(np.stack([cT[:, 0:128], np.concatenate([cT[:, 128:192]] * 2, axis=1)], axis=2))
    indices = np.linspace(0, CAD - 1, SQ).astype(np.int64)
    ca = ctx_768[:, SKE:, :]
    caS = np.ascontiguousarray(np.tile(ca[:, :, indices], (1, 3 * H0, 1)))
    caT = np.zeros((128, 2, B * NTOK), f)
    flat = ca.transpose(2, 0, 1).reshape(CAD, B * NTOK)
    caT[:, 0], caT[0:64, 1] = flat[0:128], flat[128:192]

    def kv(rows):
        w = np.zeros((128, KV_COLS), f)
        for at, m in ((W_K0, L0_xattn_Wk), (W_K1, L1_xattn_Wk), (W_V0, L0_xattn_Wv), (W_V1, L1_xattn_Wv)):
            w[:, at:at + HID] = np.asarray(m)[rows]
        return w

    first, rest = np.arange(128), np.tile(np.arange(128, 192), 2)
    w_all = np.concatenate(
        [kv(first), kv(rest)]
        + [rows3(np.asarray(w)).reshape(128, 3 * HID) for w in (L0_xattn_Wq, L1_xattn_Wq, L1_xattn_Wo)]
        + [head_rows(np.asarray(L0_xattn_Wout)).reshape(128, 4 * HID)], axis=1)
    w_ca = np.zeros((128, 2, 2 * HID), f)
    for n, m in enumerate((L0_xattn_Wk_ca, L0_xattn_Wv_ca)):
        m = np.asarray(m)
        w_ca[:, 0, n * HID:(n + 1) * HID], w_ca[0:64, 1, n * HID:(n + 1) * HID] = m[0:128], m[128:192]
    wqT = np.zeros((384, H0, 64), f)
    wqT[0:HID, :, 0:D0] = np.asarray(L0_xattn_Wq).T.reshape(HID, H0, D0)
    wqT = np.ascontiguousarray(wqT.reshape(3, 128, H0 * 64).transpose(1, 0, 2))
    bd = np.zeros((384, 3, H0, NTOK), f)
    wqca = np.asarray(L0_xattn_Wq_ca)
    for h in range(H0):
        bd[h * D0:(h + 1) * D0, :, h, :] = wqca[:, h * D0:(h + 1) * D0].T[:, None, :]
    bd96 = np.ascontiguousarray(bd.reshape(3, 128, 96).transpose(1, 0, 2))
    consts = np.zeros((128, 161), f)
    consts[:, 160] = 1
    consts[:, 0:128] = np.eye(128, dtype=f)
    for r in range(96):
        consts[r, 128 + (r % 32) // NTOK] = 1
    for r in range(HID):
        consts[r % 128, 136 + 8 * (r // 128) + r // D0] = 1
    bias = np.ascontiguousarray(np.broadcast_to(
        np.stack([np.asarray(L0_xattn_b_out), np.asarray(L1_xattn_bo)]), (SQ, 2, HID)))

    arrays = {"in_xT": xT, "in_xpad": xpad, "in_ctxT": ctxT, "in_caS": caS, "in_caT": caT, "in_w_all": w_all,
              "in_w_ca": w_ca, "in_wqT": wqT, "in_bd96": bd96, "in_consts": consts, "in_bias": bias}
    nc = bacc.Bacc("TRN2", target_bir_lowering=False, num_devices=1)
    args = [nc.dram_tensor(n, a.shape, mybir.dt.from_np(a.dtype), kind="ExternalInput").ap()
            for n, a in arrays.items()]
    out = nc.dram_tensor("out", (B, SQ, HID), F32, kind="ExternalOutput").ap()
    xattn_kernel(nc, *args, out)
    r = run_bass_kernel_spmd(nc, [arrays], core_ids=[0])
    return r.results[0]["out"]
```

```python
from contextlib import ExitStack

import concourse.bass as bass
from concourse import mybir

F32 = mybir.dt.float32
F32R = mybir.dt.float32r
ALU = mybir.AluOpType
ACT = mybir.ActivationFunctionType
AX = mybir.AxisListType.X

B, SQ, HID = 16, 112, 320
SK, CAD, NTOK = 375, 192, 4
SKE = SK - NTOK
SKP = SK + 1
H0, D0 = 8, 40
H1, D1 = 20, 16
KC, NKC = 125, 3
P = 128
SCALE0 = float(D0) ** -0.5
SCALE1 = float(D1) ** -0.5

KV_COLS = 1344
W_K0, W_K1, W_V0, W_V1 = 0, 320, 704, 1024
C_KV = 0
C_WQ0 = 2 * KV_COLS
C_WQ1 = C_WQ0 + 3 * HID
C_WO1 = C_WQ1 + 3 * HID
C_WO0 = C_WO1 + 3 * HID
C_ALL = C_WO0 + 4 * HID

UNITS = [(0, 'K1_0', 'c'), (1, 'K1_1', 'c'), (2, 'K1_2', 'c'), (3, 'V1_0', 'c'), (4, 'W2', 'n'), (5, 'V1_1', 'c'), (5, 'V1_2', 'c'), (6, 'out1', 'e'), (7, 'q0', 'n'), (8, 'S2_0', 'n'), (9, 'S2_1', 'n'), (11, 'q0T_0', 'n'), (12, 'q0T_1', 'n'), (13, 'K0_0', 'n'), (14, 'K0_1', 'n'), (15, 'out0', 'c'), (16, 'K0_2', 'n'), (17, 'T2_0', 'n'), (18, 'x1T', 'c'), (19, 'T2_1', 'n'), (20, 'q1', 'c'), (22, 'PV2', 'n'), (22, 'q1T_0', 'c'), (23, 'q1T_1', 'c'), (23, 'V0_0', 'n'), (24, 'S3', 'n'), (25, 'q1T_2', 'c'), (26, 'V0_1', 'n'), (27, 'V0_2', 'n')]
FIRST_UNITS = [(step, name, "n") for step, name in (
    (0, "W2"), (1, "q0"), (3, "K0_0"), (4, "K0_1"), (5, "K0_2"), (6, "S2_0"), (7, "S2_1"), (8, "q0T_0"), (9,
    "q0T_1"), (12, "T2_0"), (13, "T2_1"), (14, "PV2"), (15, "S3"), (16, "V0_0"), (17, "V0_1"), (18, "V0_2")
)]
HEADS = H0 + H1
LAG_T, LAG_PV = 3, 4
O0_STEP, O1_STEP = H0 + LAG_PV, LAG_PV
K0_ROWS, K1_ROWS = 120, 128
DMAS_K0, DMAS_K1 = 9, 24
PSLOTS = 4
POOL_HEADS = {"prob2": (13, 14, 15, 16), "x1b": (), "xb": (24, 26)}
NORMALISED_BY_POOL = frozenset(sum(POOL_HEADS.values(), ()))
COPIED_BY_DVE = frozenset({7, 8, 9, 11, 15, 21, 23, 24})
FIRST = 3
GQ_STEPS = (9, 11, 12, 13)
TOKEN_STEP = 8
SPLIT_STEPS = (2, 14, 16, 17)
PER_TWO_UNITS, PER_TWO_HEADS = 2 * len(UNITS), 2 * HEADS


def groups_of(t):
    return (("n" if t < B - 1 else "") + ("c" if 0 <= t < B else "") + ("l" if 1 <= t <= B else "")
            + ("e" if t >= 2 else ""))


def steps_of(t):
    return ([*range(H0)] if "c" in groups_of(t) else []) + ([*range(H0, HEADS)] if "l" in groups_of(t) else [])


class Iteration:

    def __init__(self, t0, j=0):
        self.t0, self.j, self.t = t0, j, t0 + 2 * j
        self.groups = groups_of(t0)
        self.present = [(s, u) for s, u, g in (UNITS if t0 >= 0 else FIRST_UNITS) if g in self.groups]
        before = sum(g in groups_of(t) for t in range(-1, t0) for _, _, g in UNITS)
        self.at = {u: before + i for i, (_, u) in enumerate(self.present)}
        self.head_at = {s: sum(len(steps_of(t)) for t in range(t0)) + i for i, s in enumerate(steps_of(t0))}
        self.before = Iteration(t0 - 1, j) if t0 >= 0 else None

    def of(self, step):
        return (self, step) if step >= 0 or self.before is None else (self.before, step + HEADS)

    def units(self, step):
        it, step = self.of(step)
        return [(it, u) for s, u in it.present if s == step]

    def head(self, step):
        it, step = self.of(step)
        return (it, step) if step in it.head_at else None

    def heads(self, step, more=0):
        return self.head_at[step] + 1 + more + PER_TWO_HEADS * self.j

    def bank_heads(self, step, more=0):
        return self.head_at[step] // 2 + 1 + more + HEADS * self.j

    def slot_heads(self, step):
        return self.head_at[step] // PSLOTS + 1 + PER_TWO_HEADS // PSLOTS * self.j

    def batches(self, per, off, extra=0):
        return per * (self.t0 + off) + extra + 2 * per * self.j

    def bank(self, unit):
        return self.at[unit] % 2

    def filled(self, unit):
        return self.at[unit] + 1 + PER_TWO_UNITS * self.j

    def drained(self, unit):
        return self.at[unit] // 2 + 1 + len(UNITS) * self.j

    def parity(self, off):
        return (self.t0 + off) % 2

    def pairs(self, per, off):
        return per * ((self.t0 + off) // 2 + 1) + per * self.j


def xattn_kernel(nc, xT, xpad, ctxT, caS, caT, w_all, w_ca, wqT, bd96, consts, bias, out):
    scratch = nc.dram_tensor("v3_rows", [B * NTOK, H0 * 64], F32, kind="Internal").ap()

    with ExitStack() as ctx:
        def sb(name, shape, dt=F32):
            return ctx.enter_context(nc.sbuf_tensor(name, shape, dt))

        def pb(name, shape):
            return ctx.enter_context(nc.psum_tensor(name, shape, F32))

        def sem(name):
            return ctx.enter_context(nc.semaphore(name))

        WH = sb("WH", [P, C_ALL], F32R)
        WL = sb("WL", [P, C_ALL], F32R)
        arena = sb("arena", [P, 4416])
        stage = sb("stage", [P, 4, NKC, SKP])
        prob = arena[:, 0:PSLOTS * SKP].rearrange("p (s n) -> p s n", s=PSLOTS)
        probT = arena[:, 1504:2176].rearrange("p (s k q) -> p s k q", s=2, k=NKC)
        prob2 = arena[:, 2176:3072].rearrange("p (h k) -> p h k", h=H0)
        prob2T = arena[:, 3072:3968].rearrange("p (h q) -> p h q", h=H0)
        hs1T = arena[:, 3968:4416].rearrange("p (c q) -> p c q", c=4)
        k1_hi, k1_lo, k0_hi, k0_lo = (stage[:, i] for i in range(4))
        k0_stack = sb("k0_stack", [K0_ROWS, H0, SKP], F32R)
        k1_stack = [sb(f"k1_stack{i}", [K1_ROWS, H1 // 2, SKP], F32R) for i in range(2)]
        v0 = sb("v0", [P, NKC, H0 * 64])
        v1 = [sb(f"v1_{i}", [P, NKC, H1 * 32]) for i in range(2)]
        ctx_raw = sb("ctx_raw", [P, 2, SKP])
        ctx_hi = sb("ctx_hi", [P, 2, SKP], F32R)
        ctx_lo = sb("ctx_lo", [P, SKP], F32R)
        x_raw = sb("x_raw", [P, 3, SQ])
        x_hi = sb("x_hi", [P, 3, SQ], F32R)
        x_lo = sb("x_lo", [P, 2, SQ], F32R)
        qn = sb("qn", [SQ, H1 * 64], F32R)
        q0T = sb("q0T", [K0_ROWS, H0, SQ], F32R)
        q1T = [sb(f"q1T{i}", [P, H1 // 2, SQ], F32R) for i in range(2)]
        xp = sb("xp", [SQ, H0 * 64])
        act_hi = sb("act_hi", [P, 4, SQ], F32R)
        act_lo = sb("act_lo", [P, 4, SQ], F32R)
        x1 = sb("x1", [SQ, HID])
        x1b = [sb(f"x1b{i}", [SQ, HID]) for i in range(2)]
        xb = sb("xb", [SQ, HID])
        bias_sb = sb("bias_sb", [SQ, 2, HID])
        gq = sb("gq", [P, 4, B * 32])
        gb = sb("gb", [P, 4, 32])
        ca_raw = sb("ca_raw", [96, SQ])
        ca_st = sb("ca_st", [96, SQ], F32R)
        w2s = sb("w2s", [96, SQ], F32R)
        w2bd = sb("w2bd", [96, H0, SQ], F32R)
        bd = sb("bd", [P, 3, 96])
        cst = sb("cst", [P, 161])
        one = cst[:, 160:161]
        ident = cst[:, 0:128]
        mask96 = cst[0:96, 128:136]
        mask3 = cst[:, 136:160].rearrange("p (c h) -> p c h", c=3)
        caT_sb = gb[:, :, :].rearrange("p (a c) n -> p a (c n)", a=2)
        negmax = sb("negmax", [SQ, HEADS])
        psum_ = sb("psum_", [SQ, HEADS])
        rsum = sb("rsum", [SQ, HEADS])
        negmax2 = sb("negmax2", [SQ, H0])
        sum2 = sb("sum2", [SQ, H0])
        rsum2 = sb("rsum2", [SQ, H0])
        p3 = sb("p3", [SQ, H0, NTOK])
        negmax3 = sb("negmax3", [SQ, H0])
        sum3 = sb("sum3", [SQ, H0])
        rsum3 = sb("rsum3", [SQ, H0])
        outb = x1b

        wca = gq[:, 0:3, :].rearrange("p m n -> p (m n)")[:, 0:1280].rearrange("p (a n) -> p a n", a=2)
        stage_flat = stage[:, :, :, :].rearrange("p a c n -> p (a c n)")
        wqT_sb = stage_flat[:, 0:1536].rearrange("p (c n) -> p c n", c=3)
        k2bd = v1[0][:, :, 0:512]

        def weight_part(i, whole):
            if i in (1, 3):
                kv = whole[:, C_KV:C_WQ0].rearrange("p (c n) -> p c n", c=2)
                return kv[:, :, W_K0:W_K0 + HID] if i == 1 else kv[:, :, W_K1:KV_COLS]
            return whole[:, {0: slice(C_WQ0, C_WQ1), 2: slice(C_WQ1, C_WO0), 4: slice(C_WO0, C_ALL)}[i]].unsqueeze(1)

        raw_weights = [
            arena[:, 0:3 * HID].unsqueeze(1),
            arena[:, 3 * HID:5 * HID].rearrange("p (c n) -> p c n", c=2),
            v1[1][:, :, :].rearrange("p k n -> p (k n)").unsqueeze(1),
            stage_flat[:, 0:2 * (KV_COLS - W_K1)].rearrange("p (c n) -> p c n", c=2),
            arena[:, 0:4 * HID].unsqueeze(1),
        ]

        bankS = [pb(f"bankS{i}", [P, 512]) for i in range(2)]
        bankT = [pb(f"bankT{i}", [P, 512]) for i in range(2)]
        bankO0 = pb("bankO0", [P, 512])
        bankO1 = pb("bankO1", [P, 512])
        bankX = [pb(f"bankX{i}", [P, 512]) for i in range(2)]
        gq_banks = [bankS[0], bankS[1], bankO0, bankO1]

        w_loaded = [sem(f"w_loaded{i}") for i in range(5)]
        w_ca_loaded = sem("w_ca_loaded")
        w_qT_loaded = sem("w_qT_loaded")
        bd_loaded = sem("bd_loaded")
        bias_loaded = sem("bias_loaded")
        const_loaded = sem("const_loaded")
        w_rounded = sem("w_rounded")
        w_split = sem("w_split")
        zeroed = sem("zeroed")
        pro_pe = sem("pro_pe")
        pro_vec = sem("pro_vec")
        v3_stored = sem("v3_stored")
        x_loaded = sem("x_loaded")
        ca_loaded = sem("ca_loaded")
        ctx_loaded = sem("ctx_loaded")
        xp_loaded = sem("xp_loaded")
        v3_loaded = sem("v3_loaded")
        k0_stacked = sem("k0_stacked")
        k1_stacked = [sem(f"k1_stacked{i}") for i in range(2)]
        scores_done = sem("scores_done")
        max_done = sem("max_done")
        exp_done = sem("exp_done")
        rsum_done = sem("rsum_done")
        prob_ready = [sem(f"prob_ready{i}") for i in range(PSLOTS)]
        probT_done = sem("probT_done")
        probT_copied = [sem(f"probT_copied{i}") for i in range(2)]
        pv_done = sem("pv_done")
        unit_filled = sem("unit_filled")
        bank_drained = [sem(f"bank_drained{i}") for i in range(2)]
        k1_rounded = sem("k1_rounded")
        k0_rounded = sem("k0_rounded")
        q0_rounded = sem("q0_rounded")
        q1_rounded = sem("q1_rounded")
        w2_rounded = sem("w2_rounded")
        x1T_rounded = sem("x1T_rounded")
        o0_rounded = sem("o0_rounded")
        o1_rounded = sem("o1_rounded")
        o0_split = sem("o0_split")
        o1_split = sem("o1_split")
        ca_split = sem("ca_split")
        w2_expanded = sem("w2_expanded")
        x_split = sem("x_split")
        ctx_split = sem("ctx_split")
        gb_copied = sem("gb_copied")
        xb_ready = sem("xb_ready")
        x1b_ready = sem("x1b_ready")
        max2_done = sem("max2_done")
        rsum2_done = sem("rsum2_done")
        prob2_ready = sem("prob2_ready")
        p3_vec = sem("p3_vec")
        exp3_done = sem("exp3_done")
        p3_ready = sem("p3_ready")
        out_stored = sem("out_stored")
        pool_chain = sem("pool_chain")

        def whole_run(eng, iteration):
            for t in range(-1, FIRST):
                iteration(Iteration(t))
            with eng.Fori(0, (B - 1 - FIRST) // 2) as j:
                iteration(Iteration(FIRST, j))
                iteration(Iteration(FIRST + 1, j))
            for t in range(B - 1, B + 2):
                iteration(Iteration(t))

        block = ctx.enter_context(nc.Block())

        @block.sync
        def _(sp):
            def load_weights(i):
                sp.dma_start(raw_weights[i], weight_part(i, w_all)).then_inc(w_loaded[i], 16)

            sp.dma_start(cst[:, :], consts).then_inc(const_loaded, 16)
            sp.dma_start(bd[:, :, :], bd96).then_inc(bd_loaded, 16)

            xT_cols = xT.rearrange("b p c q -> p b (c q)")
            caS_cols = caS.rearrange("b p q -> p b q")
            xp_cols = xpad.rearrange("b p n -> p b n")
            ctx_cols = ctxT.rearrange("b p c n -> p b (c n)")

            def iteration(it):
                if "n" in it.groups:
                    n = it.t + 1
                    if "c" in it.groups:
                        sp.wait_ge(xb_ready, it.batches(1, 1))
                    sp.dma_start(x_raw[:, :, :].rearrange("p c q -> p (c q)").unsqueeze(1),
                                 xT_cols[:, bass.ds(n, 1), :]).then_inc(x_loaded, 16)
                    sp.dma_start(ca_raw[:, :].unsqueeze(1), caS_cols[:, bass.ds(n, 1), :]).then_inc(ca_loaded, 16)
                    if "c" not in it.groups:
                        load_weights(0)
                    sp.dma_start(ctx_raw[:, :, :].rearrange("p c n -> p (c n)").unsqueeze(1),
                                 ctx_cols[:, bass.ds(n, 1), :]).then_inc(ctx_loaded, 16)
                    if "c" not in it.groups:
                        load_weights(1)
                        sp.dma_start(caT_sb, caT).then_inc(w_ca_loaded, 16)
                        sp.dma_start(wca, w_ca).then_inc(w_ca_loaded, 16)
                        sp.dma_start(wqT_sb, wqT).then_inc(w_qT_loaded, 16)
                    sp.dma_start(xp[:, :].unsqueeze(1), xp_cols[:, bass.ds(n, 1), :]).then_inc(xp_loaded, 16)
                    if "c" not in it.groups:
                        load_weights(2)
                        sp.dma_start(bias_sb[:, :, :], bias).then_inc(bias_loaded, 16)
                        sp.wait_ge(pro_vec, 2)
                        sp.dma_start(scratch, v0[0:B * NTOK, 0, :]).then_inc(v3_stored, 16)
                        sp.wait_ge(pro_pe, 6)
                        load_weights(3)
                        sp.wait_ge(w_split, 2)
                        load_weights(4)
                if "c" in it.groups:
                    dst = k1_stack[it.parity(0)]
                    sp.wait_ge(bank_drained[it.bank("K1_2")], it.drained("K1_2"))
                    for r in range(8):
                        nch = 3 if r < 4 else 2
                        for part, src in enumerate((k1_lo, k1_hi, k1_hi)):
                            to = 64 * (r % 2) + D1 * part
                            sp.dma_start(dst[to:to + D1, r // 2:r // 2 + 4 * (nch - 1) + 1:4, :].bitcast(F32),
                                         src[D1 * r:D1 * r + D1, 0:nch, :])\
                                .then_inc(k1_stacked[it.parity(0)], 16)
                if "n" in it.groups:
                    sp.wait_ge(bank_drained[it.bank("K0_2")], it.drained("K0_2"))
                    for r in range(3):
                        nch = 3 if r < 2 else 2
                        for part, src in enumerate((k0_lo, k0_hi, k0_hi)):
                            to = D0 * part
                            sp.dma_start(k0_stack[to:to + D0, r:r + 3 * (nch - 1) + 1:3, :].bitcast(F32),
                                         src[D0 * r:D0 * r + D0, 0:nch, :]).then_inc(k0_stacked, 16)
                    if "c" not in it.groups:
                        sp.wait_ge(v3_stored, 16)
                    sp.dma_start(v0[KC - NTOK:KC, NKC - 1, :], scratch[bass.ds(n * NTOK, NTOK), :])\
                        .then_inc(v3_loaded, 16)

            whole_run(sp, iteration)

        @block.gpsimd
        def _(pool):
            nc.gpsimd.memset(v0[:, :, :], 0.0).then_inc(zeroed, 1)
            nc.gpsimd.memset(qn[:, :].bitcast(F32), 0.0).then_inc(zeroed, 1)

            def rounded(hi, src):
                rows, cols = src.shape
                return nc.gpsimd.tensor_tensor(hi, src, one[0:rows, :].broadcast_to((rows, cols)), ALU.mult)

            def expand_w2(it):
                pool.wait_ge(bank_drained[it.bank("W2")], it.drained("W2"))
                pool.wait_ge(x_split if "c" in it.groups else ctx_split, it.batches(1, 1, 1))
                nc.gpsimd.tensor_tensor(
                    w2bd[:, :, :], w2s[:, :].bitcast(F32).unsqueeze(1).broadcast_to((96, H0, SQ)),
                    mask96.unsqueeze(2).broadcast_to((96, H0, SQ)), ALU.mult).then_inc(w2_expanded, 1)

            def split_ctx(it):
                pool.wait_ge(ctx_loaded, it.batches(16, 1, 16))
                if "c" in it.groups:
                    pool.wait_ge(unit_filled, it.filled("V1_2"))
                pool.wait_ge(w2_expanded if "c" in it.groups else x_split, it.batches(1, 1, 1))
                rounded(ctx_hi[:, :, :].rearrange("p c n -> p (c n)"),
                        ctx_raw[:, :, :].rearrange("p c n -> p (c n)")).then_inc(pool_chain, 1)
                pool.wait_ge(pool_chain, it.batches(5, 1, 4))
                nc.gpsimd.tensor_tensor(ctx_lo[:, :], ctx_raw[:, 0, :], ctx_hi[:, 0, :].bitcast(F32),
                                        ALU.subtract).then_inc(pool_chain, 1)
                pool.wait_ge(pool_chain, it.batches(5, 1, 5))
                nc.gpsimd.tensor_tensor(ctx_hi[64:128, 1, :], ctx_raw[64:128, 1, :],
                                        ctx_hi[64:128, 1, :].bitcast(F32), ALU.subtract).then_inc(ctx_split, 1)

            def normalise(it, after):
                if "l" in it.groups:
                    for s in POOL_HEADS[after]:
                        slot = prob[0:SQ, s % PSLOTS, 0:SK]
                        pool.wait_ge(rsum_done, it.heads(s))
                        nc.gpsimd.tensor_tensor(slot, slot, rsum[:, s:s + 1].broadcast_to((SQ, SK)), ALU.mult)\
                            .then_inc(prob_ready[s % PSLOTS], 1)

            def iteration(it):
                if "n" in it.groups:
                    if "c" not in it.groups:
                        pool.wait_ge(const_loaded, 16)
                    pool.wait_ge(ca_loaded, it.batches(16, 1, 16))
                    if "c" in it.groups:
                        pool.wait_ge(max2_done, it.batches(2, 1))
                    rounded(ca_st[:, :], ca_raw[:, :]).then_inc(pool_chain, 1)
                    pool.wait_ge(pool_chain, it.batches(5, 1, 1))
                    nc.gpsimd.tensor_tensor(ca_st[32:64, :], ca_raw[32:64, :], ca_st[32:64, :].bitcast(F32),
                                            ALU.subtract).then_inc(ca_split, 1)
                    pool.wait_ge(x_loaded, it.batches(16, 1, 16))
                    pool.wait_ge(ca_split, it.batches(1, 1, 1))
                    if "c" in it.groups:
                        pool.wait_ge(q0_rounded, it.batches(1, 1))
                    rounded(x_hi[:, :, :].rearrange("p c q -> p (c q)"),
                            x_raw[:, :, :].rearrange("p c q -> p (c q)")).then_inc(pool_chain, 1)
                    pool.wait_ge(pool_chain, it.batches(5, 1, 2))
                    nc.gpsimd.tensor_tensor(x_lo[:, :, :], x_raw[:, 0:2, :], x_hi[:, 0:2, :].bitcast(F32),
                                            ALU.subtract).then_inc(pool_chain, 1)
                    pool.wait_ge(pool_chain, it.batches(5, 1, 3))
                    nc.gpsimd.tensor_tensor(x_hi[64:128, 2, :], x_raw[64:128, 2, :],
                                            x_hi[64:128, 2, :].bitcast(F32), ALU.subtract).then_inc(x_split, 1)
                    if "c" in it.groups:
                        expand_w2(it)
                        split_ctx(it)
                    else:
                        split_ctx(it)
                        expand_w2(it)
                if "e" in it.groups:
                    pool.wait_ge(bank_drained[it.bank("out1")], it.drained("out1"))
                    pool.dma_start(out[bass.ds(it.t - 2, 1)].rearrange("a q n -> q (a n)"),
                                   outb[it.parity(-2)][:, :]).then_inc(out_stored, 16)
                if "n" in it.groups:
                    pool.wait_ge(rsum2_done, it.batches(1, 1, 1))
                    pool.wait_ge(ctx_split if "c" in it.groups else w2_expanded, it.batches(1, 1, 1))
                    nc.gpsimd.tensor_tensor(prob2[0:SQ], prob2[0:SQ],
                                            rsum2[:, :].unsqueeze(2).broadcast_to((SQ, H0, SQ)),
                                            ALU.mult).then_inc(prob2_ready, 1)
                normalise(it, "prob2")
                if "c" in it.groups:
                    pool.wait_ge(bank_drained[it.bank("out0")], it.drained("out0"))
                    if it.t0 >= 2:
                        pool.wait_ge(out_stored, it.batches(16, -1))
                    if "n" in it.groups:
                        pool.wait_ge(prob2_ready, it.batches(1, 1, 1))
                    nc.gpsimd.tensor_tensor(x1b[it.parity(0)][:, :], x1[:, :], bias_sb[:, 1, :], ALU.add)\
                        .then_inc(x1b_ready, 1)
                normalise(it, "x1b")
                if "n" in it.groups:
                    pool.wait_ge(xp_loaded, it.batches(16, 1, 16))
                    if "c" not in it.groups:
                        pool.wait_ge(bias_loaded, 16)
                    pool.wait_ge(unit_filled, it.filled("PV2"))
                    if "c" in it.groups:
                        pool.wait_ge(x1b_ready, it.batches(1, 0, 1))
                    nc.gpsimd.tensor_tensor(
                        xb[:, :].rearrange("p (h d) -> p h d", h=H0),
                        xp[:, :].rearrange("p (h d) -> p h d", h=H0)[:, :, 0:D0],
                        bias_sb[:, 0, :].rearrange("p (h d) -> p h d", h=H0), ALU.add).then_inc(xb_ready, 1)
                normalise(it, "xb")
                if "c" not in it.groups and "n" in it.groups:
                    pool.wait_ge(pro_pe, 6)
                    nc.gpsimd.memset(v1[0][:, :, :], 0.0).then_inc(zeroed, 1)
                    pool.wait_ge(w_split, 3)
                    nc.gpsimd.memset(v1[1][:, :, :], 0.0).then_inc(zeroed, 1)

            whole_run(pool, iteration)
            pool.wait_ge(out_stored, 16 * B)

        @block.scalar
        def _(act):
            def round_weights(i):
                act.wait_ge(w_loaded[i], 16)
                nc.scalar.activation(weight_part(i, WH), raw_weights[i], ACT.Copy).then_inc(w_rounded, 1)

            round_weights(0)

            def exps2(it, half):
                act.wait_ge(max2_done, it.batches(2, 1, half + 1))
                X = bankX[it.bank(f"S2_{half}")]
                for h in range(4 * half, 4 * half + 4):
                    last = nc.scalar.activation(prob2[0:SQ, h, :], X[0:SQ, (h % 4) * SQ:(h % 4 + 1) * SQ], ACT.Exp,
                                                bias=negmax2[:, h:h + 1], accum_out=sum2[:, h:h + 1])
                last.then_inc(bank_drained[it.bank(f"S2_{half}")], 1)

            def unit(it, u):
                X = bankX[it.bank(u)]
                free = bank_drained[it.bank(u)]
                kind, _, i = u.partition("_")
                i = int(i or 0)
                if kind in ("S2", "S3", "out0", "out1"):
                    return
                act.wait_ge(unit_filled, it.filled(u))
                if kind == "K1":
                    if i == 0 and it.t0 >= 1:
                        act.wait_ge(k1_stacked[it.parity(-1)], it.pairs(16 * DMAS_K1, -1))
                    rows = P if i < 2 else 64
                    nc.scalar.activation(k1_hi[0:rows, i, :].bitcast(F32R), X[0:rows, 0:SKP], ACT.Copy)\
                        .then_inc(k1_rounded, 1)
                elif kind == "K0":
                    if i == 0 and it.t0 >= 0:
                        act.wait_ge(k0_stacked, it.batches(16 * DMAS_K0, 1))
                    rows = 120 if i < 2 else 80
                    nc.scalar.activation(k0_hi[0:rows, i, :].bitcast(F32R), X[0:rows, 0:SKP], ACT.Copy)\
                        .then_inc(k0_rounded, 1)
                elif kind == "V0":
                    rows = KC if i < 2 else KC - NTOK
                    if it.t0 < 0:
                        act.wait_ge(v3_stored, 16)
                    nc.scalar.activation(v0[0:rows, i, :].rearrange("p (h d) -> p h d", h=H0)[:, :, 0:D0],
                                         X[0:rows, 0:HID].rearrange("p (h d) -> p h d", h=H0), ACT.Copy)\
                        .then_inc(free, 1)
                elif kind == "V1":
                    if i == 0 and it.t0 < 2:
                        act.wait_ge(zeroed, 3 + it.t0)
                    if i == 0 and "e" in it.groups:
                        act.wait_ge(pv_done, it.before.heads(HEADS - 1))
                    dst = v1[it.parity(0)][0:KC, i, :].rearrange("p (g a d) -> p g a d", a=4, d=D1)
                    src = X[0:KC, 0:HID].rearrange("p (g a d) -> p g a d", a=2, d=D1)
                    nc.scalar.activation(dst[:, :, 0:4:3, :], src, ACT.Copy).then_inc(free, 1)
                elif kind == "q0":
                    dst = qn[:, 0:H0 * 120].rearrange("p (h a d) -> p h a d", h=H0, a=3)[:, :, 0:3:2, :]
                    src = X[0:SQ, 0:HID].rearrange("p (h d) -> p h d", h=H0).unsqueeze(2)
                    nc.scalar.activation(dst, src.broadcast_to((SQ, H0, 2, D0)), ACT.Copy, scale=SCALE0)\
                        .then_inc(q0_rounded, 1)
                elif kind == "q1":
                    dst = qn[:, :].rearrange("p (h a d) -> p h a d", h=H1, a=4)[:, :, 0:3:2, :]
                    src = X[0:SQ, 0:HID].rearrange("p (h d) -> p h d", h=H1).unsqueeze(2)
                    nc.scalar.activation(dst, src.broadcast_to((SQ, H1, 2, D1)), ACT.Copy, scale=SCALE1)\
                        .then_inc(q1_rounded, 1)
                elif kind == "q0T":
                    nc.scalar.activation(q0T[:, 4 * i:4 * i + 4, :].rearrange("p h q -> p (h q)"),
                                         X[0:K0_ROWS, 0:4 * SQ], ACT.Copy).then_inc(free, 1)
                elif kind == "q1T":
                    g = 4 if i < 2 else 2
                    nc.scalar.activation(q1T[it.parity(0)][:, 4 * i:4 * i + g, :].rearrange("p h q -> p (h q)"),
                                         X[:, 0:g * SQ], ACT.Copy).then_inc(free, 1)
                elif kind == "W2":
                    nc.scalar.activation(w2s[:, :], X[0:96, 0:SQ], ACT.Copy, scale=SCALE0).then_inc(w2_rounded, 1)
                elif kind == "T2":
                    nc.scalar.activation(prob2T[0:SQ, 4 * i:4 * i + 4, :].rearrange("p h q -> p (h q)"),
                                         X[0:SQ, 0:4 * SQ], ACT.Copy).then_inc(free, 1)
                    if i == 1:
                        if it.t0 < 0:
                            act.wait_ge(pro_vec, 6)
                        nc.scalar.activation(gb[:, :, :], gq[:, :, bass.ds((it.t + 1) * 32, 32)], ACT.Copy)\
                            .then_inc(gb_copied, 1)
                elif kind == "PV2":
                    nc.scalar.activation(hs1T.rearrange("p c q -> p (c q)"), X[:, 0:4 * SQ], ACT.Copy)\
                        .then_inc(free, 1)
                elif kind == "x1T":
                    nc.scalar.activation(act_hi[:, 0:2, :].rearrange("p c q -> p (c q)"), X[:, 0:2 * SQ], ACT.Copy)
                    nc.scalar.activation(act_hi[0:64, 2, :], X[0:64, 2 * SQ:3 * SQ], ACT.Copy)\
                        .then_inc(x1T_rounded, 1)

            def iteration(it):
                for s in range(HEADS):
                    if it.t0 < 0 and s in SPLIT_STEPS:
                        round_weights(1 + SPLIT_STEPS.index(s))
                    if s == O0_STEP and "c" in it.groups:
                        act.wait_ge(pv_done, it.heads(H0 - 1))
                        nc.scalar.activation(act_hi[:, :, :].rearrange("p c q -> p (c q)"), bankO0[:, 0:4 * SQ],
                                             ACT.Copy).then_inc(o0_rounded, 1)
                    if s == O1_STEP and "e" in it.groups:
                        act.wait_ge(pv_done, it.before.heads(HEADS - 1))
                        nc.scalar.activation(act_hi[:, 0:2, :].rearrange("p c q -> p (c q)"),
                                             bankO1[:, 0:2 * SQ], ACT.Copy)
                        nc.scalar.activation(act_hi[0:64, 2, :], bankO1[0:64, 2 * SQ:3 * SQ], ACT.Copy)\
                            .then_inc(o1_rounded, 1)
                    for at, u in it.units(s - 1):
                        unit(at, u)
                    for at, u in it.units(s - 2):
                        if u == "S2_0":
                            exps2(at, 0)
                        elif u == "S2_1":
                            exps2(at, 1)
                        elif u == "S3":
                            act.wait_ge(bank_drained[at.bank("S3")], at.drained("S3"))
                            nc.scalar.activation(p3[:, :, :], p3[:, :, :], ACT.Exp).then_inc(exp3_done, 1)
                    if it.head(s - LAG_T) and (s - LAG_T) % HEADS not in COPIED_BY_DVE:
                        at, h = it.head(s - LAG_T)
                        act.wait_ge(probT_done, at.heads(h))
                        if at.head_at[h] >= 2:
                            act.wait_ge(pv_done, at.heads(h, -2))
                        nc.scalar.activation(probT[0:KC, h % 2], bankT[h % 2][0:KC, 0:NKC * SQ]
                                             .rearrange("p (k q) -> p k q", k=NKC), ACT.Copy)\
                            .then_inc(probT_copied[h % 2], 1)
                    if it.head(s):
                        act.wait_ge(max_done, it.heads(s))
                        keys = SKE if s < H0 else SK
                        nc.scalar.activation(prob[0:SQ, s % PSLOTS, 0:keys], bankS[s % 2][0:SQ, 0:keys], ACT.Exp,
                                             bias=negmax[:, s:s + 1], accum_out=psum_[:, s:s + 1])\
                            .then_inc(exp_done, 1)

            whole_run(act, iteration)

        @block.vector
        def _(dve):
            def split_weights(i):
                dve.wait_ge(w_rounded, i + 1)
                nc.vector.tensor_tensor(weight_part(i, WL), raw_weights[i], weight_part(i, WH).bitcast(F32),
                                        ALU.subtract).then_inc(w_split, 1)

            split_weights(0)

            def drain_token_products():
                dve.wait_ge(const_loaded, 16)
                dve.wait_ge(pro_pe, 1)
                for c in range(3):
                    rows = P if c < 2 else 64
                    last = nc.vector.tensor_tensor(
                        k2bd[0:rows, c].rearrange("p (h n) -> p h n", h=H0),
                        bankT[0][0:rows, c * 64:c * 64 + 64].unsqueeze(1).broadcast_to((rows, H0, B * NTOK)),
                        mask3[0:rows, c, :].unsqueeze(2).broadcast_to((rows, H0, B * NTOK)), ALU.mult)
                last.then_inc(pro_vec, 1)
                dve.wait_ge(zeroed, 2)
                dve.wait_ge(pro_pe, 2)
                nc.vector.tensor_copy(v0[0:B * NTOK, 0, :].rearrange("p (h d) -> p h d", h=H0)[:, :, 0:D0],
                                      bankT[1][0:B * NTOK, 0:HID].rearrange("p (h d) -> p h d", h=H0))\
                    .then_inc(pro_vec, 1)

            def drain_query_keys(m):
                dve.wait_ge(pro_pe, 3 + m)
                nc.vector.tensor_scalar(gq[:, m, :].rearrange("p (b h k) -> p h b k", b=B, h=H0),
                                        gq_banks[m][:, :].rearrange("p (h b k) -> p h b k", h=H0, b=B), SCALE0, None,
                                        ALU.mult).then_inc(pro_vec, 1)

            def scaled_lo(dst, src, scale, hi):
                return nc.vector.scalar_tensor_tensor(out=dst, in0=src, scalar=scale, in1=hi, op0=ALU.mult,
                                                      op1=ALU.subtract)

            def unit(it, u):
                X = bankX[it.bank(u)]
                free = bank_drained[it.bank(u)]
                kind, _, i = u.partition("_")
                i = int(i or 0)
                if kind == "K1":
                    dve.wait_ge(k1_rounded, it.batches(3, 0, i + 1))
                    rows = P if i < 2 else 64
                    nc.vector.tensor_tensor(k1_lo[0:rows, i, :].bitcast(F32R), X[0:rows, 0:SKP],
                                            k1_hi[0:rows, i, :], ALU.subtract).then_inc(free, 1)
                elif kind == "K0":
                    dve.wait_ge(k0_rounded, it.batches(3, 1, i + 1))
                    rows = 120 if i < 2 else 80
                    nc.vector.tensor_tensor(k0_lo[0:rows, i, :].bitcast(F32R), X[0:rows, 0:SKP],
                                            k0_hi[0:rows, i, :], ALU.subtract).then_inc(free, 1)
                elif kind == "q0":
                    dve.wait_ge(q0_rounded, it.batches(1, 1, 1))
                    parts = qn[:, 0:H0 * 120].rearrange("p (h a d) -> p h a d", h=H0, a=3)
                    scaled_lo(parts[:, :, 1, :], X[0:SQ, 0:HID].rearrange("p (h d) -> p h d", h=H0), SCALE0,
                              parts[:, :, 0, :].bitcast(F32)).then_inc(free, 1)
                elif kind == "q1":
                    dve.wait_ge(q1_rounded, it.batches(1, 0, 1))
                    parts = qn[:, :].rearrange("p (h a d) -> p h a d", h=H1, a=4)
                    scaled_lo(parts[:, :, 1, :], X[0:SQ, 0:HID].rearrange("p (h d) -> p h d", h=H1), SCALE1,
                              parts[:, :, 0, :].bitcast(F32)).then_inc(free, 1)
                elif kind == "W2":
                    dve.wait_ge(w2_rounded, it.batches(1, 1, 1))
                    scaled_lo(w2s[64:96, :], X[64:96, 0:SQ], SCALE0, w2s[64:96, :].bitcast(F32)).then_inc(free, 1)
                elif kind == "S2":
                    dve.wait_ge(unit_filled, it.filled(u))
                    nc.vector.tensor_reduce(negmax2[:, 4 * i:4 * i + 4],
                                            X[0:SQ, 0:4 * SQ].rearrange("p (h k) -> p h k", h=4), axis=AX,
                                            op=ALU.max, negate=True).then_inc(max2_done, 1)
                elif kind == "S3":
                    dve.wait_ge(unit_filled, it.filled(u))
                    sc = X[0:SQ, 0:H0 * NTOK].rearrange("p (h k) -> p h k", h=H0)
                    nc.vector.tensor_reduce(negmax3[:, :], sc, axis=AX, op=ALU.max, negate=True)\
                        .then_inc(p3_vec, 1)
                    dve.wait_ge(p3_vec, it.batches(3, 1, 1))
                    nc.vector.tensor_tensor(p3[:, :, :], sc,
                                            negmax3[:, :].unsqueeze(2).broadcast_to((SQ, H0, NTOK)), ALU.add)\
                        .then_inc(free, 1)
                elif kind == "out0":
                    dve.wait_ge(unit_filled, it.filled(u))
                    dve.wait_ge(xb_ready, it.batches(1, 0, 1))
                    if it.t0 >= 1:
                        dve.wait_ge(x1b_ready, it.batches(1, 0))
                    nc.vector.tensor_tensor(x1[:, :], X[0:SQ, 0:HID], xb[:, :], ALU.add).then_inc(free, 1)
                elif kind == "x1T":
                    dve.wait_ge(x1T_rounded, it.batches(1, 0, 1))
                    nc.vector.tensor_tensor(act_lo[:, 0:2, :].rearrange("p c q -> p (c q)"), X[:, 0:2 * SQ],
                                            act_hi[:, 0:2, :].rearrange("p c q -> p (c q)").bitcast(F32),
                                            ALU.subtract)
                    nc.vector.tensor_tensor(act_hi[64:128, 2, :], X[0:64, 2 * SQ:3 * SQ],
                                            act_hi[0:64, 2, :].bitcast(F32), ALU.subtract).then_inc(free, 1)
                elif kind == "out1":
                    dve.wait_ge(unit_filled, it.filled(u))
                    y = x1b[it.parity(-2)]
                    dve.wait_ge(x1b_ready, it.batches(1, -2, 1))
                    nc.vector.tensor_tensor(y[:, :], X[0:SQ, 0:HID], y[:, :], ALU.add).then_inc(free, 1)

            def iteration(it):
                for s in range(HEADS):
                    if it.t0 < 0 and s in SPLIT_STEPS:
                        split_weights(1 + SPLIT_STEPS.index(s))
                    if it.t0 < 0 and s == TOKEN_STEP:
                        drain_token_products()
                    if it.t0 < 0 and s - 1 in GQ_STEPS:
                        drain_query_keys(GQ_STEPS.index(s - 1))
                    if it.head(s):
                        dve.wait_ge(scores_done, it.heads(s))
                        keys = SKE if s < H0 else SK
                        nc.vector.tensor_reduce(negmax[:, s:s + 1], bankS[s % 2][0:SQ, 0:keys], axis=AX, op=ALU.max,
                                                negate=True).then_inc(max_done, 1)
                    if it.head(s - 1):
                        at, h = it.head(s - 1)
                        dve.wait_ge(exp_done, at.heads(h))
                        nc.vector.reciprocal(rsum[:, h:h + 1], psum_[:, h:h + 1]).then_inc(rsum_done, 1)
                    if it.head(s - LAG_T) and (s - LAG_T) % HEADS in COPIED_BY_DVE:
                        at, h = it.head(s - LAG_T)
                        dve.wait_ge(probT_done, at.heads(h))
                        if at.head_at[h] >= 2:
                            dve.wait_ge(pv_done, at.heads(h, -2))
                        nc.vector.tensor_copy(probT[0:KC, h % 2], bankT[h % 2][0:KC, 0:NKC * SQ]
                                              .rearrange("p (k q) -> p k q", k=NKC)).then_inc(probT_copied[h % 2], 1)
                    if s == O0_STEP and "c" in it.groups:
                        dve.wait_ge(o0_rounded, it.batches(1, 0, 1))
                        nc.vector.tensor_tensor(act_lo[:, :, :].rearrange("p c q -> p (c q)"), bankO0[:, 0:4 * SQ],
                                                act_hi[:, :, :].rearrange("p c q -> p (c q)").bitcast(F32),
                                                ALU.subtract).then_inc(o0_split, 1)
                    if s == O1_STEP and "e" in it.groups:
                        dve.wait_ge(o1_rounded, it.batches(1, -2, 1))
                        nc.vector.tensor_tensor(act_lo[:, 0:2, :].rearrange("p c q -> p (c q)"),
                                                bankO1[:, 0:2 * SQ],
                                                act_hi[:, 0:2, :].rearrange("p c q -> p (c q)").bitcast(F32),
                                                ALU.subtract)
                        nc.vector.tensor_tensor(act_hi[64:128, 2, :], bankO1[0:64, 2 * SQ:3 * SQ],
                                                act_hi[0:64, 2, :].bitcast(F32), ALU.subtract).then_inc(o1_split, 1)
                    for at, u in it.units(s - 1):
                        unit(at, u)
                    for at, u in it.units(s - 3):
                        if u == "S2_1":
                            dve.wait_ge(bank_drained[at.bank("S2_0")], at.drained("S2_0"))
                            dve.wait_ge(bank_drained[at.bank("S2_1")], at.drained("S2_1"))
                            nc.vector.reciprocal(rsum2[:, :], sum2[:, :]).then_inc(rsum2_done, 1)
                        if u == "S3":
                            dve.wait_ge(exp3_done, at.batches(1, 1, 1))
                            nc.vector.reduce_sum(sum3[:, :], p3[:, :, :], axis=AX).then_inc(p3_vec, 1)
                            dve.wait_ge(p3_vec, at.batches(3, 1, 2))
                            nc.vector.reciprocal(rsum3[:, :], sum3[:, :]).then_inc(p3_vec, 1)
                            dve.wait_ge(p3_vec, at.batches(3, 1, 3))
                            nc.vector.tensor_tensor(p3[:, :, :], p3[:, :, :],
                                                    rsum3[:, :].unsqueeze(2).broadcast_to((SQ, H0, NTOK)), ALU.mult)\
                                .then_inc(p3_ready, 1)
                    if it.head(s - 1) and (s - 1) % HEADS not in NORMALISED_BY_POOL:
                        at, h = it.head(s - 1)
                        keys = SKE if h < H0 else SK
                        slot = prob[0:SQ, h % PSLOTS, :]
                        if h < H0:
                            if h == 0:
                                dve.wait_ge(p3_ready, at.batches(1, 0, 1))
                            if at.head_at[h] >= PSLOTS:
                                dve.wait_ge(probT_done, at.heads(h, -PSLOTS))
                            nc.vector.tensor_copy(slot[:, SKE:SK], p3[:, h, :])
                        dve.wait_ge(rsum_done, at.heads(h))
                        nc.vector.tensor_scalar(slot[:, 0:keys], slot[:, 0:keys], rsum[:, h:h + 1], None,
                                                ALU.mult).then_inc(prob_ready[h % PSLOTS], 1)

            whole_run(dve, iteration)

        @block.tensor
        def _(pe):
            pe.wait_ge(const_loaded, 16)
            def token_products():
                pe.wait_ge(w_ca_loaded, 32)
                for c in range(3):
                    m = P if c < 2 else 64
                    for a in range(2):
                        k = P if a == 0 else 64
                        last = nc.tensor.matmul(bankT[0][0:m, c * 64:c * 64 + 64], wca[0:k, a, c * P:c * P + m],
                                                caT_sb[0:k, a, :], start=(a == 0), stop=(a == 1))
                last.then_inc(pro_pe, 1)
                for a in range(2):
                    k = P if a == 0 else 64
                    last = nc.tensor.matmul(bankT[1][0:64, 0:HID], caT_sb[0:k, a, :], wca[0:k, a, HID:2 * HID],
                                            start=(a == 0), stop=(a == 1))
                last.then_inc(pro_pe, 1)

            spans = [(0, 0, 4, True, False), (1, 3, 4, False, True), (1, 4, 7, True, False), (2, 6, 7, False, True),
                     (2, 7, 8, True, True)]

            def query_keys(m):
                if m == 0:
                    pe.wait_ge(w_qT_loaded, 16)
                    pe.wait_ge(pro_vec, 1)
                for c, h0, h1, start, stop in spans:
                    k = P if c < 2 else 64
                    cols = slice(h0 * B * NTOK, h1 * B * NTOK)
                    last = nc.tensor.matmul(gq_banks[m][:, cols], wqT_sb[0:k, c, m * P:m * P + P], k2bd[0:k, c, cols],
                                            start=start, stop=stop)
                last.then_inc(pro_pe, 1)

            def in_parts(dst, passes):
                for n, (lhs, rhs) in enumerate(passes):
                    last = nc.tensor.matmul(dst, lhs, rhs, start=(n == 0), stop=(n == len(passes) - 1))
                return last

            def unit(it, u):
                X = bankX[it.bank(u)]
                kind, _, i = u.partition("_")
                i = int(i or 0)
                if it.t0 > -1 or it.at[u] >= 2:
                    pe.wait_ge(bank_drained[it.bank(u)], it.drained(u) - 1)
                if kind in ("K0", "K1"):
                    if i == 0 and kind == "K0":
                        pe.wait_ge(ctx_split, it.batches(1, 1, 1))
                        if it.t0 < 0:
                            pe.wait_ge(w_split, 2)
                    lo, m = (W_K1 + P * i, P) if kind == "K1" else (W_K0 + 120 * i, 120 if i < 2 else 80)
                    a, b = slice(lo, lo + m), slice(KV_COLS + lo, KV_COLS + lo + m)
                    last = in_parts(X[0:m, 0:SKP], [
                        (WH[:, a], ctx_hi[:, 0, :]), (WH[:, a], ctx_lo[:, :]), (WL[:, a], ctx_hi[:, 0, :]),
                        (WH[:, b], ctx_hi[:, 1, :]), (WL[:, b], ctx_hi[:, 1, :])])
                elif kind in ("V0", "V1"):
                    lo = W_V0 if kind == "V0" else W_V1
                    a, b = slice(lo, lo + HID), slice(KV_COLS + lo, KV_COLS + lo + HID)
                    k = slice(KC * i, KC * i + KC)
                    if it.t0 < 0 and i == 0:
                        pe.wait_ge(w_split, 4)
                    last = in_parts(X[0:KC, 0:HID], [
                        (ctx_hi[:, 0, k], WH[:, a]), (ctx_lo[:, k], WH[:, a]), (ctx_hi[:, 0, k], WL[:, a]),
                        (ctx_hi[:, 1, k], WH[:, b]), (ctx_hi[:, 1, k], WL[:, b])])
                elif kind in ("q0", "q1", "out1"):
                    if kind == "q0":
                        pe.wait_ge(x_split, it.batches(1, 1, 1))
                        if it.t0 < 0:
                            pe.wait_ge(w_split, 1)
                        hi, lo, w = x_hi, x_lo, C_WQ0
                    elif kind == "q1":
                        pe.wait_ge(bank_drained[it.bank("x1T")], it.drained("x1T"))
                        hi, lo, w = act_hi, act_lo, C_WQ1
                    else:
                        pe.wait_ge(o1_split, it.batches(1, -2, 1))
                        hi, lo, w = act_hi, act_lo, C_WO1
                    w0, w1, w2 = (slice(w + HID * c, w + HID * c + HID) for c in range(3))
                    last = in_parts(X[0:SQ, 0:HID], [
                        (hi[:, 0, :], WH[:, w0]), (hi[:, 0, :], WL[:, w0]), (lo[:, 0, :], WH[:, w0]),
                        (hi[:, 1, :], WH[:, w1]), (hi[:, 1, :], WL[:, w1]), (lo[:, 1, :], WH[:, w1]),
                        (hi[:, 2, :], WH[:, w2]), (hi[:, 2, :], WL[:, w2])])
                elif kind == "out0":
                    pe.wait_ge(o0_split, it.batches(1, 0, 1))
                    if it.t0 == 0:
                        pe.wait_ge(w_split, 5)
                    passes = []
                    for c in range(4):
                        w = slice(C_WO0 + HID * c, C_WO0 + HID * c + HID)
                        passes += [(act_hi[:, c, :], WH[:, w]), (act_hi[:, c, :], WL[:, w]),
                                   (act_lo[:, c, :], WH[:, w])]
                    last = in_parts(X[0:SQ, 0:HID], passes)
                elif kind == "q0T":
                    if i == 0:
                        pe.wait_ge(bank_drained[it.bank("q0")], it.drained("q0"))
                    for h in range(4):
                        c = 120 * (4 * i + h)
                        last = nc.tensor.transpose(X[0:K0_ROWS, h * SQ:h * SQ + SQ],
                                                   qn[:, c:c + 120].bitcast(F32), ident[0:SQ, 0:SQ])
                elif kind == "q1T":
                    if i == 0:
                        pe.wait_ge(bank_drained[it.bank("q1")], it.drained("q1"))
                    for g in range(4 if i < 2 else 2):
                        c = 128 * (4 * i + g)
                        last = nc.tensor.transpose(X[:, g * SQ:g * SQ + SQ],
                                                   qn[:, c:c + 128].bitcast(F32), ident[0:SQ, 0:SQ])
                elif kind == "x1T":
                    pe.wait_ge(bank_drained[it.bank("out0")], it.drained("out0"))
                    for c in range(3):
                        m = P if c < 2 else 64
                        last = nc.tensor.transpose(X[0:m, c * SQ:c * SQ + SQ], x1[:, c * P:c * P + m],
                                                   ident[0:SQ, 0:SQ])
                elif kind == "W2":
                    pe.wait_ge(x_loaded, it.batches(16, 1, 16))
                    if it.t0 < 0:
                        pe.wait_ge(bd_loaded, 16)
                    for c in range(3):
                        k = P if c < 2 else 64
                        last = nc.tensor.matmul(X[0:96, 0:SQ], bd[0:k, c, :], x_raw[0:k, c, :],
                                                start=(c == 0), stop=(c == 2))
                elif kind == "S2":
                    if i == 0:
                        pe.wait_ge(ca_split, it.batches(1, 1, 1))
                        pe.wait_ge(w2_expanded, it.batches(1, 1, 1))
                    last = nc.tensor.matmul(X[0:SQ, 0:4 * SQ], ca_st[:, :],
                                            w2bd[:, 4 * i:4 * i + 4, :].rearrange("p h q -> p (h q)"),
                                            start=True, stop=True)
                elif kind == "T2":
                    if i == 0:
                        pe.wait_ge(prob2_ready, it.batches(1, 1, 1))
                    for h in range(4):
                        last = nc.tensor.transpose(X[0:SQ, h * SQ:h * SQ + SQ], prob2[0:SQ, 4 * i + h, :],
                                                   ident[0:SQ, 0:SQ])
                elif kind == "PV2":
                    pe.wait_ge(xp_loaded, it.batches(16, 1, 16))
                    pe.wait_ge(bank_drained[it.bank("T2_0")], it.drained("T2_0"))
                    pe.wait_ge(bank_drained[it.bank("T2_1")], it.drained("T2_1"))
                    for h in range(H0):
                        last = nc.tensor.matmul(X[64 * (h % 2):64 * (h % 2) + 64, (h // 2) * SQ:(h // 2 + 1) * SQ],
                                                xp[:, 64 * h:64 * h + 64], prob2T[0:SQ, h, :],
                                                start=True, stop=True)
                elif kind == "S3":
                    pe.wait_ge(bank_drained[it.bank("PV2")], it.drained("PV2"))
                    pe.wait_ge(gb_copied, it.batches(1, 1, 1))
                    for c in range(4):
                        last = nc.tensor.matmul(X[0:SQ, 0:32], hs1T[:, c, :], gb[:, c, :], start=(c == 0),
                                                stop=(c == 3))
                last.then_inc(unit_filled, 1)

            def scores(it, s):
                if it.head_at[s] >= 2:
                    pe.wait_ge(exp_done, it.heads(s, -2))
                if s < H0:
                    if s == 0:
                        pe.wait_ge(k0_stacked, it.batches(16 * DMAS_K0, 0, 16 * DMAS_K0))
                    nc.tensor.matmul(bankS[s % 2][0:SQ, 0:SKE + 1], q0T[:, s, :], k0_stack[:, s, 0:SKE + 1],
                                     start=True, stop=True).then_inc(scores_done, 1)
                else:
                    h, par = s - H0, it.parity(-1)
                    if h == 0:
                        pe.wait_ge(k1_stacked[par], it.pairs(16 * DMAS_K1, -1))
                    row = slice(64 * (h % 2), 64 * (h % 2) + 3 * D1)
                    nc.tensor.matmul(bankS[s % 2][0:SQ, 0:SKP], q1T[par][row, h // 2, :],
                                     k1_stack[par][row, h // 2, :], start=True, stop=True)\
                        .then_inc(scores_done, 1)

            def transposes(it, s):
                pe.wait_ge(prob_ready[s % PSLOTS], it.slot_heads(s))
                if it.head_at[s] >= 2:
                    pe.wait_ge(probT_copied[s % 2], it.bank_heads(s, -1))
                for k in range(NKC):
                    last = nc.tensor.transpose(bankT[s % 2][0:KC, k * SQ:(k + 1) * SQ],
                                               prob[0:SQ, s % PSLOTS, KC * k:KC * k + KC], ident[0:SQ, 0:SQ])
                last.then_inc(probT_done, 1)

            def attend(it, s):
                pe.wait_ge(probT_copied[s % 2], it.bank_heads(s))
                if s < H0:
                    if s == 0:
                        pe.wait_ge(v3_loaded, it.batches(16, 0, 16))
                        if it.t0 >= 1:
                            pe.wait_ge(o0_split, it.batches(1, 0))
                    dst, c = bankO0[64 * (s % 2):64 * (s % 2) + 64, (s // 2) * SQ:(s // 2 + 1) * SQ], 64 * s
                    for k in range(NKC):
                        last = nc.tensor.matmul(dst, v0[0:KC, k, c:c + 64], probT[0:KC, s % 2, k, :],
                                                start=(k == 0), stop=(k == NKC - 1))
                else:
                    h = s - H0
                    g = h // 2
                    if h == 0 and it.t0 >= 2:
                        pe.wait_ge(o1_split, it.batches(1, -1))
                    dst = bankO1[32 * (g % 4):32 * (g % 4) + 32, (g // 4) * SQ:(g // 4 + 1) * SQ]
                    for k in range(NKC):
                        last = nc.tensor.matmul(dst, v1[it.parity(-1)][0:KC, k, 32 * h:32 * h + 32],
                                                probT[0:KC, s % 2, k, :], start=(h % 2 == 0 and k == 0),
                                                stop=(h % 2 == 1 and k == NKC - 1))
                last.then_inc(pv_done, 1)

            def iteration(it):
                for s in range(HEADS):
                    if it.t0 < 0 and s == TOKEN_STEP:
                        token_products()
                    if it.t0 < 0 and s in GQ_STEPS:
                        query_keys(GQ_STEPS.index(s))
                    if it.head(s):
                        scores(it, s)
                    if it.head(s - LAG_T):
                        transposes(*it.head(s - LAG_T))
                    if it.head(s - LAG_PV):
                        attend(*it.head(s - LAG_PV))
                    for at, u in it.units(s):
                        unit(at, u)

            whole_run(pe, iteration)


def kernel(x, ctx_768, L0_xattn_Wq, L0_xattn_Wk, L0_xattn_Wv, L0_xattn_Wq_ca, L0_xattn_Wk_ca, L0_xattn_Wv_ca,
           L0_xattn_Wout, L0_xattn_b_out, L1_xattn_Wq, L1_xattn_Wk, L1_xattn_Wv, L1_xattn_Wo, L1_xattn_bo):
    import numpy as np
    import concourse.bacc as bacc
    from concourse.bass_utils import run_bass_kernel_spmd

    f = np.float32

    def rows3(w):
        return np.stack([w[..., 0:128, :], w[..., 128:256, :],
                         np.concatenate([w[..., 256:320, :]] * 2, axis=-2)], axis=-2)

    def head_rows(w):
        p = np.zeros((H0, 64) + w.shape[1:], f)
        p[:, 0:D0] = w.reshape((H0, D0) + w.shape[1:])
        return p.reshape((4, 128) + w.shape[1:]).transpose(1, 0, 2)

    x, ctx_768 = np.asarray(x), np.asarray(ctx_768)
    xT = np.ascontiguousarray(rows3(x.transpose(0, 2, 1)).reshape(B, 128, 3, SQ))
    xpad = np.zeros((B, SQ, H0, 64), f)
    xpad[..., 0:D0] = x.reshape(B, SQ, H0, D0)
    xpad = xpad.reshape(B, SQ, H0 * 64)
    cT = np.zeros((B, CAD, SKP), f)
    cT[:, :, 0:SK] = ctx_768.transpose(0, 2, 1)
    ctxT = np.ascontiguousarray(np.stack([cT[:, 0:128], np.concatenate([cT[:, 128:192]] * 2, axis=1)], axis=2))
    indices = np.linspace(0, CAD - 1, SQ).astype(np.int64)
    ca = ctx_768[:, SKE:, :]
    caS = np.ascontiguousarray(np.tile(ca[:, :, indices], (1, 3 * H0, 1)))
    caT = np.zeros((128, 2, B * NTOK), f)
    flat = ca.transpose(2, 0, 1).reshape(CAD, B * NTOK)
    caT[:, 0], caT[0:64, 1] = flat[0:128], flat[128:192]

    def kv(rows):
        w = np.zeros((128, KV_COLS), f)
        for at, m in ((W_K0, L0_xattn_Wk), (W_K1, L1_xattn_Wk), (W_V0, L0_xattn_Wv), (W_V1, L1_xattn_Wv)):
            w[:, at:at + HID] = np.asarray(m)[rows]
        return w

    first, rest = np.arange(128), np.tile(np.arange(128, 192), 2)
    w_all = np.concatenate(
        [kv(first), kv(rest)]
        + [rows3(np.asarray(w)).reshape(128, 3 * HID) for w in (L0_xattn_Wq, L1_xattn_Wq, L1_xattn_Wo)]
        + [head_rows(np.asarray(L0_xattn_Wout)).reshape(128, 4 * HID)], axis=1)
    w_ca = np.zeros((128, 2, 2 * HID), f)
    for n, m in enumerate((L0_xattn_Wk_ca, L0_xattn_Wv_ca)):
        m = np.asarray(m)
        w_ca[:, 0, n * HID:(n + 1) * HID], w_ca[0:64, 1, n * HID:(n + 1) * HID] = m[0:128], m[128:192]
    wqT = np.zeros((384, H0, 64), f)
    wqT[0:HID, :, 0:D0] = np.asarray(L0_xattn_Wq).T.reshape(HID, H0, D0)
    wqT = np.ascontiguousarray(wqT.reshape(3, 128, H0 * 64).transpose(1, 0, 2))
    bd = np.zeros((384, 3, H0, NTOK), f)
    wqca = np.asarray(L0_xattn_Wq_ca)
    for h in range(H0):
        bd[h * D0:(h + 1) * D0, :, h, :] = wqca[:, h * D0:(h + 1) * D0].T[:, None, :]
    bd96 = np.ascontiguousarray(bd.reshape(3, 128, 96).transpose(1, 0, 2))
    consts = np.zeros((128, 161), f)
    consts[:, 160] = 1
    consts[:, 0:128] = np.eye(128, dtype=f)
    for r in range(96):
        consts[r, 128 + (r % 32) // NTOK] = 1
    for r in range(HID):
        consts[r % 128, 136 + 8 * (r // 128) + r // D0] = 1
    bias = np.ascontiguousarray(np.broadcast_to(
        np.stack([np.asarray(L0_xattn_b_out), np.asarray(L1_xattn_bo)]), (SQ, 2, HID)))

    arrays = {"in_xT": xT, "in_xpad": xpad, "in_ctxT": ctxT, "in_caS": caS, "in_caT": caT, "in_w_all": w_all,
              "in_w_ca": w_ca, "in_wqT": wqT, "in_bd96": bd96, "in_consts": consts, "in_bias": bias}
    nc = bacc.Bacc("TRN2", target_bir_lowering=False, num_devices=1)
    args = [nc.dram_tensor(n, a.shape, mybir.dt.from_np(a.dtype), kind="ExternalInput").ap()
            for n, a in arrays.items()]
    out = nc.dram_tensor("out", (B, SQ, HID), F32, kind="ExternalOutput").ap()
    xattn_kernel(nc, *args, out)
    r = run_bass_kernel_spmd(nc, [arrays], core_ids=[0])
    return r.results[0]["out"]
```
